# Optimizing a Trainium2 kernel written in Bass

```python
import numpy as np
import jax
import jax.numpy as jnp

def _softmax(x, axis=-1):
    return jax.nn.softmax(x, axis=axis)

def _gelu(x):
    return jax.nn.gelu(x, approximate=True)

def _silu(x):
    return jax.nn.silu(x)

def _sigmoid(x):
    return jax.nn.sigmoid(x)

def _layernorm(x, axis=-1, eps=1e-05):
    m = jnp.mean(x, axis=axis, keepdims=True)
    v = jnp.var(x, axis=axis, keepdims=True)
    return (x - m) / jnp.sqrt(v + eps)

def _scatter_add(tgt, idx, src, axis=0):
    return tgt.at[idx].add(src)

def _segment_sum(src, seg, n):
    return jax.ops.segment_sum(src, seg, n)
kernel_name = 'mk_prb_d2_jaxref_r4_73667d'

def setup_inputs(seed: int=0):
    np.random.seed(seed)
    _w = jnp.asarray

    def _L0_attn_setup():
        import jax, jax.numpy as jnp
        import numpy as np
        EMB, HEADS = (256, 16)
        S = EMB // HEADS
        key = jax.random.key(seed)
        ks = jax.random.split(key, 7)
        b, t = (2, 512)
        sc = 0.02
        return {'x': jax.random.normal(ks[0], (b, t, EMB), jnp.float32), 'W_down': jax.random.normal(ks[1], (EMB, EMB), jnp.float32) * sc, 'tokeys': jax.random.normal(ks[2], (HEADS, S, S), jnp.float32) * sc, 'toqueries': jax.random.normal(ks[3], (HEADS, S, S), jnp.float32) * sc, 'tovalues': jax.random.normal(ks[4], (HEADS, S, S), jnp.float32) * sc, 'W_unify': jax.random.normal(ks[5], (EMB, EMB), jnp.float32) * sc, 'b_unify': jax.random.normal(ks[6], (EMB,), jnp.float32) * sc}
    _L0_attn_in = _L0_attn_setup()

    def _L0_ffn_setup():
        import jax, jax.numpy as jnp
        import numpy as np
        N_EXPERTS = 16
        TOPK = 2
        CAPACITY_FACTOR = 1.0
        EPS_GATE = 1e-06
        LN_EPS = 1e-05
        key = jax.random.key(seed)
        ks = jax.random.split(key, 8)
        B, S, D, F, E = (4, 512, 256, 1024, N_EXPERTS)
        Fp = F // E
        s = 0.02
        return {'x': jax.random.normal(ks[0], (B, S, D), dtype=jnp.float32), 'wg': s * jax.random.normal(ks[1], (D, E), dtype=jnp.float32), 'bg': jnp.zeros((E,), dtype=jnp.float32), 'w1': s * jax.random.normal(ks[2], (E, D, Fp), dtype=jnp.float32), 'b1': jnp.zeros((E, Fp), dtype=jnp.float32), 'w2': s * jax.random.normal(ks[3], (E, Fp, D), dtype=jnp.float32), 'b2': jnp.zeros((E, D), dtype=jnp.float32), 'gamma': jnp.ones((D,), dtype=jnp.float32), 'beta': jnp.zeros((D,), dtype=jnp.float32)}
    _L0_ffn_in = _L0_ffn_setup()

    def _L1_attn_setup():
        import jax, jax.numpy as jnp
        import numpy as np
        from jax import lax
        B, T, D, H, K = (4, 512, 256, 1024, 3)
        EPS = 1e-06

        def _rmsnorm(z, w):
            return z * lax.rsqrt(jnp.mean(z * z, axis=-1, keepdims=True) + EPS) * w
        key = jax.random.key(seed)
        ks = jax.random.split(key, 12)
        return {'x': jax.random.normal(ks[0], (B, T, D), jnp.float32), 'norm_w': jnp.ones((D,), jnp.float32), 'conv_w': jax.random.normal(ks[1], (D, 1, K), jnp.float32) * 0.1, 'conv_b': jax.random.normal(ks[2], (D,), jnp.float32) * 0.01, 'a': jnp.tanh(jax.random.normal(ks[3], (D,), jnp.float32)), 'b': jax.random.normal(ks[4], (D,), jnp.float32), 'mlp_norm_w': jnp.ones((D,), jnp.float32), 'w_gate': jax.random.normal(ks[5], (D, H), jnp.float32) * D ** (-0.5), 'b_gate': jnp.zeros((H,), jnp.float32), 'w_up': jax.random.normal(ks[6], (D, H), jnp.float32) * D ** (-0.5), 'b_up': jnp.zeros((H,), jnp.float32), 'w_down': jax.random.normal(ks[7], (H, D), jnp.float32) * H ** (-0.5), 'b_down': jnp.zeros((D,), jnp.float32)}
    _L1_attn_in = _L1_attn_setup()

    def _L1_ffn_setup():
        import jax, jax.numpy as jnp
        import numpy as np
        B, T, C, E, K, CAP, H = (8, 512, 256, 8, 2, 1024, 1024)
        key = jax.random.key(seed)
        ks = jax.random.split(key, 6)
        s = 0.02
        return {'x': jax.random.normal(ks[0], (B, T, C), jnp.float32), 'rw1': s * jax.random.normal(ks[1], (C, H), jnp.float32), 'rb1': jnp.zeros((H,), jnp.float32), 'rw2': s * jax.random.normal(ks[2], (H, E), jnp.float32), 'rb2': jnp.zeros((E,), jnp.float32), 'ew1': s * jax.random.normal(ks[3], (E, C, H), jnp.float32), 'eb1': jnp.zeros((E, H), jnp.float32), 'ew2': s * jax.random.normal(ks[4], (E, H, C), jnp.float32), 'eb2': jnp.zeros((E, C), jnp.float32)}
    _L1_ffn_in = _L1_ffn_setup()
    _d = {'L0_attn_x': _L0_attn_in['x'], 'L0_attn_W_down': _L0_attn_in['W_down'], 'L0_attn_tokeys': _L0_attn_in['tokeys'], 'L0_attn_toqueries': _L0_attn_in['toqueries'], 'L0_attn_tovalues': _L0_attn_in['tovalues'], 'L0_attn_W_unify': _L0_attn_in['W_unify'], 'L0_attn_b_unify': _L0_attn_in['b_unify'], 'L0_ffn_wg': _L0_ffn_in['wg'], 'L0_ffn_bg': _L0_ffn_in['bg'], 'L0_ffn_w1': _L0_ffn_in['w1'], 'L0_ffn_b1': _L0_ffn_in['b1'], 'L0_ffn_w2': _L0_ffn_in['w2'], 'L0_ffn_b2': _L0_ffn_in['b2'], 'L0_ffn_gamma': _L0_ffn_in['gamma'], 'L0_ffn_beta': _L0_ffn_in['beta'], 'L1_attn_norm_w': _L1_attn_in['norm_w'], 'L1_attn_conv_w': _L1_attn_in['conv_w'], 'L1_attn_conv_b': _L1_attn_in['conv_b'], 'L1_attn_a': _L1_attn_in['a'], 'L1_attn_b': _L1_attn_in['b'], 'L1_attn_mlp_norm_w': _L1_attn_in['mlp_norm_w'], 'L1_attn_w_gate': _L1_attn_in['w_gate'], 'L1_attn_b_gate': _L1_attn_in['b_gate'], 'L1_attn_w_up': _L1_attn_in['w_up'], 'L1_attn_b_up': _L1_attn_in['b_up'], 'L1_attn_w_down': _L1_attn_in['w_down'], 'L1_attn_b_down': _L1_attn_in['b_down'], 'L1_ffn_rw1': _L1_ffn_in['rw1'], 'L1_ffn_rb1': _L1_ffn_in['rb1'], 'L1_ffn_rw2': _L1_ffn_in['rw2'], 'L1_ffn_rb2': _L1_ffn_in['rb2'], 'L1_ffn_ew1': _L1_ffn_in['ew1'], 'L1_ffn_eb1': _L1_ffn_in['eb1'], 'L1_ffn_ew2': _L1_ffn_in['ew2'], 'L1_ffn_eb2': _L1_ffn_in['eb2']}
    _x0 = _d['L0_attn_x']
    _d['L0_attn_x'] = jax.random.normal(jax.random.fold_in(jax.random.key(seed), 1), (1, 4096, 256), dtype=_x0.dtype)
    del _x0
    return _d

def reference(L0_attn_x, L0_attn_W_down, L0_attn_tokeys, L0_attn_toqueries, L0_attn_tovalues, L0_attn_W_unify, L0_attn_b_unify, L0_ffn_wg, L0_ffn_bg, L0_ffn_w1, L0_ffn_b1, L0_ffn_w2, L0_ffn_b2, L0_ffn_gamma, L0_ffn_beta, L1_attn_norm_w, L1_attn_conv_w, L1_attn_conv_b, L1_attn_a, L1_attn_b, L1_attn_mlp_norm_w, L1_attn_w_gate, L1_attn_b_gate, L1_attn_w_up, L1_attn_b_up, L1_attn_w_down, L1_attn_b_down, L1_ffn_rw1, L1_ffn_rb1, L1_ffn_rw2, L1_ffn_rb2, L1_ffn_ew1, L1_ffn_eb1, L1_ffn_ew2, L1_ffn_eb2):

    def _L0_attn_ref(x, W_down, tokeys, toqueries, tovalues, W_unify, b_unify):
        import jax, jax.numpy as jnp
        import numpy as np
        EMB, HEADS = (256, 16)
        S = EMB // HEADS
        b, t, e = x.shape
        h, s = (HEADS, S)
        scale = s ** (-0.25)
        xd = (x @ W_down).reshape(b, t, h, s)
        keys = jnp.einsum('bthk,hik->bthi', xd, tokeys) * scale
        queries = jnp.einsum('bthk,hik->bthi', xd, toqueries) * scale
        values = jnp.einsum('bthk,hik->bthi', xd, tovalues)
        dot = jnp.einsum('bqhs,bkhs->bhqk', queries, keys)
        attn = jax.nn.softmax(dot, axis=-1)
        out = jnp.einsum('bhqk,bkhs->bqhs', attn, values).reshape(b, t, e)
        return out @ W_unify + b_unify

    def _L0_ffn_ref(x, wg, bg, w1, b1, w2, b2, gamma, beta):
        import jax, jax.numpy as jnp
        import numpy as np
        N_EXPERTS = 16
        TOPK = 2
        CAPACITY_FACTOR = 1.0
        EPS_GATE = 1e-06
        LN_EPS = 1e-05
        B, S, D = x.shape
        E = wg.shape[1]
        capacity = int(CAPACITY_FACTOR * B)
        scores = jax.nn.softmax(x @ wg + bg, axis=-1)
        _, top_i = jax.lax.top_k(scores, TOPK)
        mask = jax.nn.one_hot(top_i, E, dtype=scores.dtype).sum(-2)
        masked = scores * mask
        denom = masked.sum(0, keepdims=True) + EPS_GATE
        route = masked / denom * capacity
        route_e = jnp.transpose(route, (2, 0, 1))
        max_len = S // 2
        _, seq_ids = jax.lax.top_k(route_e, max_len)
        seq_ids = jnp.sort(seq_ids, axis=-1)
        b_idx = jnp.arange(B)[None, :, None]
        xg = x[b_idx, seq_ids]
        h = jnp.einsum('ebld,edf->eblf', xg, w1) + b1[:, None, None, :]
        h = jax.nn.gelu(h, approximate=False)
        out = jnp.einsum('eblf,efd->ebld', h, w2) + b2[:, None, None, :]
        outs = jnp.zeros_like(x).at[b_idx, seq_ids].add(out)
        z = x + outs
        mu = z.mean(-1, keepdims=True)
        var = ((z - mu) ** 2).mean(-1, keepdims=True)
        return (z - mu) / jnp.sqrt(var + LN_EPS) * gamma + beta

    def _L1_attn_ref(x, norm_w, conv_w, conv_b, a, b, mlp_norm_w, w_gate, b_gate, w_up, b_up, w_down, b_down):
        import jax, jax.numpy as jnp
        import numpy as np
        from jax import lax
        B, T, D, H, K = (4, 512, 256, 1024, 3)
        EPS = 1e-06

        def _rmsnorm(z, w):
            return z * lax.rsqrt(jnp.mean(z * z, axis=-1, keepdims=True) + EPS) * w
        y = _rmsnorm(x, norm_w)
        y_conv = lax.conv_general_dilated(y.transpose(0, 2, 1), conv_w, window_strides=(1,), padding=[(K // 2, K // 2)], dimension_numbers=('NCH', 'OIH', 'NCH'), feature_group_count=D) + conv_b[None, :, None]
        y_conv = y_conv.transpose(0, 2, 1)
        s = jnp.tanh(a)
        by = b * y

        def step(h, by_t):
            h = s * h + by_t
            return (h, h)
        _, y_ssm = lax.scan(step, jnp.zeros((x.shape[0], x.shape[2]), x.dtype), by.transpose(1, 0, 2))
        y_ssm = y_ssm.transpose(1, 0, 2)
        x = x + y_conv + y_ssm
        z = _rmsnorm(x, mlp_norm_w)
        h = jax.nn.silu(z @ w_gate + b_gate) * (z @ w_up + b_up)
        return x + h @ w_down + b_down

    def _L1_ffn_ref(x, rw1, rb1, rw2, rb2, ew1, eb1, ew2, eb2):
        import jax, jax.numpy as jnp
        import numpy as np
        B, T, C, E, K, CAP, H = (8, 512, 256, 8, 2, 1024, 1024)
        Bx, Tx, Cx = x.shape
        N = Bx * Tx
        logits = jax.nn.relu(x @ rw1 + rb1) @ rw2 + rb2
        vals, ids = jax.lax.top_k(logits, K)
        probs = jax.nn.softmax(vals, axis=-1)
        ids_f = ids.reshape(N * K)
        probs_f = probs.reshape(N * K)
        xr = jnp.repeat(x.reshape(N, Cx), K, axis=0)
        m = jax.nn.one_hot(ids_f, E, dtype=jnp.int32)
        pos = jnp.cumsum(m, axis=0) - 1
        pos_tok = jnp.take_along_axis(pos, ids_f[:, None], axis=1)[:, 0]
        keep = (pos_tok < CAP).astype(x.dtype)
        pos_c = jnp.clip(pos_tok, 0, CAP - 1)
        disp = jnp.zeros((E, CAP, Cx), x.dtype).at[ids_f, pos_c].add(xr * keep[:, None])
        h = jax.nn.relu(jnp.einsum('enc,ech->enh', disp, ew1) + eb1[:, None, :])
        eo = jnp.einsum('enh,ehc->enc', h, ew2) + eb2[:, None, :]
        y = eo[ids_f, pos_c] * (probs_f * keep)[:, None]
        return y.reshape(Bx, Tx, K, Cx).sum(axis=2)
    x = L0_attn_x
    xn = _layernorm(x, axis=-1)
    x = x + _L0_attn_ref(xn, L0_attn_W_down, L0_attn_tokeys, L0_attn_toqueries, L0_attn_tovalues, L0_attn_W_unify, L0_attn_b_unify) + _L0_ffn_ref(xn, L0_ffn_wg, L0_ffn_bg, L0_ffn_w1, L0_ffn_b1, L0_ffn_w2, L0_ffn_b2, L0_ffn_gamma, L0_ffn_beta)
    xn = _layernorm(x, axis=-1)
    x = x + _L1_attn_ref(xn, L1_attn_norm_w, L1_attn_conv_w, L1_attn_conv_b, L1_attn_a, L1_attn_b, L1_attn_mlp_norm_w, L1_attn_w_gate, L1_attn_b_gate, L1_attn_w_up, L1_attn_b_up, L1_attn_w_down, L1_attn_b_down) + _L1_ffn_ref(xn, L1_ffn_rw1, L1_ffn_rb1, L1_ffn_rw2, L1_ffn_rb2, L1_ffn_ew1, L1_ffn_eb1, L1_ffn_ew2, L1_ffn_eb2)
    return x

_drawn_inputs = setup_inputs


def setup_inputs(seed=0):
    import zlib

    import numpy as np

    out = dict(_drawn_inputs(seed))
    spreads = {'L0_ffn_bg': (0.0, 0.1),
     'L0_ffn_b1': (0.0, 0.578),
     'L0_ffn_b2': (0.0, 0.1),
     'L0_ffn_gamma': (1.0, 0.2),
     'L0_ffn_beta': (0.0, 0.1),
     'L1_attn_norm_w': (1.0, 0.2),
     'L1_attn_mlp_norm_w': (1.0, 0.2),
     'L1_attn_b_gate': (0.0, 0.378),
     'L1_attn_b_up': (0.0, 0.416),
     'L1_attn_b_down': (0.0, 0.347),
     'L1_ffn_rb1': (0.0, 0.468),
     'L1_ffn_rb2': (0.0, 0.1),
     'L1_ffn_eb1': (0.0, 0.8),
     'L1_ffn_eb2': (0.0, 0.555)}
    factors = {'L0_attn_W_down': 8.0,
     'L0_attn_tokeys': 8.0,
     'L0_attn_toqueries': 8.0,
     'L0_attn_tovalues': 8.0,
     'L0_attn_W_unify': 8.0,
     'L0_attn_b_unify': 5.113,
     'L1_attn_conv_b': 8.0,
     'L1_ffn_rw1': 3.063,
     'L1_ffn_rw2': 2.759,
     'L1_ffn_ew1': 3.222}
    for name, (base, spread) in spreads.items():
        noise = np.random.default_rng([zlib.crc32(name.encode()), seed]).standard_normal(out[name].shape)
        drawn = base * np.exp(spread * noise) if base else spread * noise
        out[name] = jnp.asarray(drawn.astype(out[name].dtype))
    for name, factor in factors.items():
        out[name] = (out[name] * factor).astype(out[name].dtype)
    return out
```

```python
from contextlib import ExitStack

import concourse.bass as bass
from concourse import mybir

F32 = mybir.dt.float32
F32R = mybir.dt.float32r
BF16 = mybir.dt.bfloat16
I32 = mybir.dt.int32
U32 = mybir.dt.uint32
ALU = mybir.AluOpType
ACT = mybir.ActivationFunctionType
AX = mybir.AxisListType

P = 128
T = 4096
C = 256
KC = C // P
NT = T // P
CH = 512
NCH = T // CH
TC = CH // P
HEADS = 16
D = C // HEADS
LN_EPS = 1e-5
E0 = 16
KEEP0 = T // 2
F0 = 1024
E1 = 8
CAP = 1024
HID = 1024
MH = HID // P

IDENT, SUMCOL, DIAG8, BEFORE, ONES, RESET, IOTA, EXPAND, CONSTS = 0, 128, 145, 153, 281, 409, 921, 1433, 2457


class Chain:

    def __init__(self, engine, semaphore):
        self.engine, self.semaphore, self.base, self.n = engine, semaphore, 0, 0

    def start(self, base):
        self.base, self.n = base, 0

    def __call__(self, instruction):
        self.n += 1
        instruction.then_inc(self.semaphore, 1)
        self.engine.wait_ge(self.semaphore, self.base + self.n)


class Phase:

    def __init__(self, nc, name):
        self.nc, self.name, self.stack = nc, name, ExitStack()

    def __enter__(self):
        return self

    def __exit__(self, *what):
        return self.stack.__exit__(*what)

    def sb(self, name, shape, dt=F32):
        return self.stack.enter_context(self.nc.sbuf_tensor(f"{self.name}_{name}", shape, dt))

    def ps(self, name, shape=(P, CH), dt=F32):
        return self.stack.enter_context(self.nc.psum_tensor(f"{self.name}_{name}_sums", list(shape), dt))

    def sem(self, name):
        return self.stack.enter_context(self.nc.semaphore(f"{self.name}_{name}"))

    def block(self):
        return self.stack.enter_context(self.nc.Block())


def front_phase(nc, x, w_down, head_weights, wg, bg, consts, CST, X, XN, XNT, V, SC, q_scratch, k_scratch):
    with Phase(nc, "front") as ph:
        WD = ph.sb("w_down", [P, KC, C])
        WG = ph.sb("w_gate", [P, KC, E0])
        BG = ph.sb("b_gate", [P, E0])
        HW = ph.sb("head_weights", [P, 3, KC, D])
        BLK = ph.sb("block_diagonal", [P, 3 * KC, P])
        BD = ph.sb("block_diagonal_t", [P, 3 * KC, P])
        STATS = ph.sb("stats", [P, TC, 6])
        MV = ph.sb("mean_var", [P, TC, 2])
        VAR = ph.sb("variance", [P, TC])
        STD = ph.sb("deviation", [P, TC])
        RSTD = ph.sb("rstd", [P, TC])
        XG = [ph.sb(f"xn_chunk{k}", [P, TC, C]) for k in range(2)]
        XT = [ph.sb(f"xn_t_chunk{k}", [P, KC, CH]) for k in range(2)]
        XD = ph.sb("x_down_t", [P, KC, CH])
        HI = [ph.sb(f"high{k}", [P, 4, CH], F32R) for k in range(2)]
        LO = [ph.sb(f"low{k}", [P, 4, CH], F32R) for k in range(2)]
        TP = [ph.ps(f"transposed{k}") for k in range(KC)]
        XDP = [ph.ps(f"x_down{k}") for k in range(KC)]
        QKP = [ph.ps(f"queries_keys{k}") for k in range(2)]
        VP = ph.ps("values")
        GP = ph.ps("gate")

        cst_in = ph.sem("constants_in")
        w_in = ph.sem("weights_in")
        x_in = [ph.sem(f"x_in{k}") for k in range(2)]
        ln_done = ph.sem("x_normalised")
        stats_ready = ph.sem("stats_ready")
        var_ready = ph.sem("variance_ready")
        std_ready = ph.sem("deviation_ready")
        xg_ready = ph.sem("xn_ready")
        t_ready = ph.sem("transposed_ready")
        xt_ready = ph.sem("xn_t_ready")
        stored = [ph.sem(f"xn_stored{k}") for k in range(2)]
        xd_ready = ph.sem("x_down_ready")
        xd_copied = ph.sem("x_down_copied")
        qk_ready = ph.sem("queries_keys_ready")
        hi_done = ph.sem("high_done")
        lo_done = ph.sem("low_done")
        parts_out = [ph.sem(f"parts_out{k}") for k in range(2)]
        v_ready = ph.sem("values_ready")
        v_copied = ph.sem("values_copied")
        g_ready = ph.sem("gate_ready")
        g_copied = ph.sem("gate_copied")
        blk_ready = ph.sem("blocks_ready")
        bd_ready = ph.sem("block_transposes_ready")
        bd_copied = ph.sem("block_transposes_copied")
        dchain = ph.sem("vector_chain")
        block = ph.block()

        @block.sync
        def _(sp):
            sp.dma_start(CST[:, :], consts).then_inc(cst_in, 16)
            for n, w in enumerate(head_weights):
                sp.dma_start(HW[:, n, :, :], w.rearrange("(m h) i k -> (h i) m k", m=KC)).then_inc(w_in, 16)
            sp.dma_start(WD[:, :, :], w_down.rearrange("(k p) n -> p k n", p=P)).then_inc(w_in, 16)
            sp.dma_start(WG[:, :, :], wg.rearrange("(k p) n -> p k n", p=P)).then_inc(w_in, 16)
            sp.dma_start(BG[:, :], bg.rearrange("(a n) -> a n", a=1).to_broadcast([P, E0])).then_inc(w_in, 16)
            with sp.Fori(0, NCH // 2) as i:
                for k in range(2):
                    n = 2 * i + k
                    sp.wait_ge(xg_ready, (n + 1) * TC)
                    sp.dma_start(XN[:, bass.ds(n * TC, TC), :], XG[k][:, :, :]).then_inc(stored[k], 16)
                    sp.wait_ge(xt_ready, (n + 2) * KC)
                    sp.dma_start(XNT[:, :, bass.ds(n * CH, CH)], XT[k][:, :, :]).then_inc(stored[k], 16)
                    sp.wait_ge(lo_done, (n + 1) * 4 + 2)
                    for m in range(KC):
                        for part, src in enumerate((HI[k], LO[k])):
                            for out, scratch in enumerate((q_scratch, k_scratch)):
                                sp.dma_start(scratch[part, m * P:(m + 1) * P, bass.ds(n * CH, CH)],
                                               src[:, 2 * out + m, :].bitcast(F32)).then_inc(parts_out[k], 16)
            for k in range(2):
                sp.wait_ge(stored[k], 32 * (NCH // 2) + 16)
                sp.wait_ge(parts_out[k], 128 * (NCH // 2) + 16)

        @block.gpsimd
        def _(pool):
            xr = x.rearrange("(n p) c -> p n c", p=P)
            with pool.Fori(0, NCH // 2) as i:
                for k in range(2):
                    n = 2 * i + k
                    pool.wait_ge(ln_done, n + 1)
                    pool.dma_start(X[:, bass.ds(n * TC, TC), :], xr[:, bass.ds(n * TC, TC), :]).then_inc(x_in[k], 16)

        @block.tensor
        def _(pe):
            ident = CST[:, IDENT:IDENT + P]
            pe.wait_ge(blk_ready, 3 * KC)
            for n in range(3 * KC):
                if n >= 2:
                    pe.wait_ge(bd_copied, n - 1)
                nc.tensor.transpose(QKP[n % 2][:, 0:P], BLK[:, n, :], ident).then_inc(bd_ready, 1)
            pe.wait_ge(bd_copied, 3 * KC)
            pe.wait_ge(w_in, 96)
            with pe.Fori(0, NCH // 2) as i:
                for k in range(2):
                    n = 2 * i + k
                    pe.wait_ge(xg_ready, (n + 1) * TC)
                    pe.wait_ge(xt_ready, (n + 1) * KC)
                    for m in range(KC):
                        for j in range(TC):
                            mm = nc.tensor.transpose(TP[m][:, j * P:(j + 1) * P], XG[k][:, j, m * P:(m + 1) * P],
                                                     ident)
                        mm.then_inc(t_ready, 1)
                    pe.wait_ge(xt_ready, (n + 2) * KC)
                    for m in range(KC):
                        pe.wait_ge(xd_copied, n * KC + m + 1)
                        for q in range(KC):
                            mm = nc.tensor.matmul(XDP[m][:, :], WD[:, q, m * P:(m + 1) * P], XT[k][:, q, :],
                                                  start=(q == 0), stop=(q == KC - 1))
                        mm.then_inc(xd_ready, 1)
                    pe.wait_ge(g_copied, n + 1)
                    for j in range(TC):
                        for q in range(KC):
                            mm = nc.tensor.matmul(GP[:, j * E0:(j + 1) * E0], XT[k][:, q, j * P:(j + 1) * P],
                                                  WG[:, q, :], start=(q == 0), stop=(q == KC - 1))
                    mm.then_inc(g_ready, 1)
                    pe.wait_ge(xd_copied, (n + 2) * KC)
                    for o in range(2 * KC):
                        pe.wait_ge(lo_done, n * 4 + o + 1)
                        nc.tensor.matmul(QKP[o % 2][:, :], BD[:, o, :], XD[:, o % KC, :], start=True, stop=True)\
                            .then_inc(qk_ready, 1)
                    for half in range(2):
                        pe.wait_ge(v_copied, n * 2 + half + 1)
                        for j in range(2):
                            for m in range(KC):
                                t = (2 * half + j) * P
                                mm = nc.tensor.matmul(VP[:, j * C + m * P:j * C + (m + 1) * P], XD[:, m, t:t + P],
                                                      BD[:, 2 * KC + m, :], start=True, stop=True)
                        mm.then_inc(v_ready, 1)

        @block.scalar
        def _(act):
            act.sem_inc(xt_ready, KC)
            act.sem_inc(xd_copied, KC)
            act.sem_inc(v_copied, 1)
            for k in range(2):
                act.sem_inc(stored[k], 16)
                act.sem_inc(parts_out[k], 16)
            for n in range(3 * KC):
                act.wait_ge(bd_ready, n + 1)
                nc.scalar.copy(BD[:, n, :], QKP[n % 2][:, 0:P]).then_inc(bd_copied, 1)
            with act.Fori(0, NCH // 2) as i:
                for k in range(2):
                    n = 2 * i + k
                    act.wait_ge(var_ready, n + 1)
                    nc.scalar.activation(STD[:, :], VAR[:, :], ACT.Sqrt).then_inc(std_ready, 1)
                    act.wait_ge(stored[k], 32 * i + 16)
                    for m in range(KC):
                        act.wait_ge(t_ready, n * KC + m + 1)
                        nc.scalar.copy(XT[k][:, m, :], TP[m][:, :]).then_inc(xt_ready, 1)
                    for m in range(KC):
                        act.wait_ge(xd_ready, n * KC + m + 1)
                        nc.scalar.copy(XD[:, m, :], XDP[m][:, :]).then_inc(xd_copied, 1)
                    act.wait_ge(parts_out[k], 128 * i + 16)
                    for o in range(2 * KC):
                        act.wait_ge(qk_ready, n * 4 + o + 1)
                        nc.scalar.mul(HI[k][:, o, :], QKP[o % 2][:, :], D ** -0.25).then_inc(hi_done, 1)
                    for half in range(2):
                        act.wait_ge(v_ready, n * 2 + half + 1)
                        nc.scalar.copy(V[:, bass.ds(n * TC + half * 2, 2), :].rearrange("p j c -> p (j c)"), VP[:, :])\
                            .then_inc(v_copied, 1)

        @block.vector
        def _(dve):
            link = Chain(dve, dchain)
            dve.sem_inc(ln_done, 2)
            dve.sem_inc(lo_done, 2)
            dve.sem_inc(g_copied, 1)
            dve.wait_ge(cst_in, 16)
            dve.wait_ge(w_in, 96)
            diag = CST[:, DIAG8:DIAG8 + 8].unsqueeze(2).to_broadcast([P, 8, D])
            for n in range(3 * KC):
                dense = HW[:, n // KC, n % KC, :].unsqueeze(1).to_broadcast([P, 8, D])
                nc.vector.tensor_tensor(BLK[:, n, :].rearrange("p (h k) -> p h k", k=D), dense, diag, ALU.mult)\
                    .then_inc(blk_ready, 1)
            with dve.Fori(0, NCH // 2) as i:
                link.start(i * 8)
                for k in range(2):
                    n = 2 * i + k
                    dve.wait_ge(x_in[k], (i + 1) * 16)
                    for j in range(TC):
                        ins = nc.vector.bn_stats(STATS[:, j, :], X[:, bass.ds(n * TC + j, 1), :].rearrange("p a c -> p (a c)"))
                    link(ins)
                    dve.sem_inc(stats_ready, 1)
                    for j in range(TC):
                        ins = nc.vector.bn_aggr(MV[:, j, :], STATS[:, j, :])
                    link(ins)
                    link(nc.vector.tensor_scalar(VAR[:, :], MV[:, :, 1], LN_EPS, None, ALU.add))
                    dve.sem_inc(var_ready, 1)
                    dve.wait_ge(std_ready, n + 1)
                    link(nc.vector.reciprocal(RSTD[:, :], STD[:, :]))
                    dve.wait_ge(stored[k], 32 * i + 16)
                    for j in range(TC):
                        nc.vector.tensor_scalar(XG[k][:, j, :], X[:, bass.ds(n * TC + j, 1), :].rearrange("p a c -> p (a c)"),
                                                MV[:, j, 0:1], RSTD[:, j:j + 1], ALU.subtract, ALU.mult)\
                            .then_inc(xg_ready, 1)
                    dve.sem_inc(ln_done, 1)
                    dve.wait_ge(g_ready, n + 1)
                    nc.vector.tensor_tensor(SC[:, :, bass.ds(n * TC, TC)].rearrange("p e t -> p t e"),
                                            GP[:, 0:TC * E0].rearrange("p (t e) -> p t e", e=E0),
                                            BG[:, :].unsqueeze(1).to_broadcast([P, TC, E0]), ALU.add)\
                        .then_inc(g_copied, 1)
                    for o in range(2 * KC):
                        dve.wait_ge(hi_done, n * 4 + o + 1)
                        nc.vector.scalar_tensor_tensor(LO[k][:, o, :], QKP[o % 2][:, :], D ** -0.25,
                                                       HI[k][:, o, :].bitcast(F32), ALU.mult, ALU.subtract)\
                            .then_inc(lo_done, 1)



def top_two(nc, link, CST, S, ne, low, work):
    FIRST, SECOND, EQ, REST, BEST1, BEST2, INDEX = work
    iota = CST[:, IOTA:IOTA + ne * NT].rearrange("p (e t) -> p e t", t=NT)

    def per_token(a):
        return a[:, :].unsqueeze(1).to_broadcast([P, ne, NT])

    def over_experts(a):
        return a[:, :, :].rearrange("p e t -> p t e")

    for scores, best, hot in ((S, BEST1, FIRST), (REST, BEST2, SECOND)):
        link(nc.vector.tensor_reduce(best[:, :], over_experts(scores), AX.X, ALU.max))
        link(nc.vector.tensor_tensor(EQ[:, :, :], scores[:, :, :], per_token(best), ALU.is_equal))
        link(nc.vector.scalar_tensor_tensor(EQ[:, :, :], iota, -64.0, EQ[:, :, :], ALU.add, ALU.mult))
        link(nc.vector.tensor_reduce(INDEX[:, :], over_experts(EQ), AX.X, ALU.min))
        link(nc.vector.scalar_tensor_tensor(hot[:, :, :], iota, -64.0, per_token(INDEX), ALU.add, ALU.is_equal))
        if hot is FIRST:
            link(nc.vector.scalar_tensor_tensor(REST[:, :, :], hot[:, :, :], low, S[:, :, :], ALU.mult, ALU.add))

class Ranks:

    def __init__(self, ph, ne):
        self.ne = ne
        self.BEFORE_P, self.TOTAL_P = ph.ps("before_in_tile"), ph.ps("tile_totals")
        self.TOTAL = ph.sb("tile_totals_sb", [P, ne * NT])
        self.SUM = ph.sb("tile_sums", [P, ne * NT])
        self.mask_ready, self.counted = ph.sem("rank_mask_ready"), ph.sem("rank_counted")

    def count(self, nc, pe, CST, MASK):
        w = self.ne * NT
        pe.wait_ge(self.mask_ready, 1)
        mask = MASK[:, :, :].rearrange("p e t -> p (e t)")
        nc.tensor.matmul(self.BEFORE_P[:, 0:w], CST[:, BEFORE:BEFORE + P], mask, start=True, stop=True)
        nc.tensor.matmul(self.TOTAL_P[:, 0:w], CST[:, ONES:ONES + P], mask, start=True, stop=True)\
            .then_inc(self.counted, 1)

    def finish(self, nc, dve, link, CST, RANK):
        w = self.ne * NT
        dve.wait_ge(self.counted, 1)
        rank = RANK[:, :, :].rearrange("p e t -> p (e t)")
        link(nc.vector.tensor_copy(self.TOTAL[:, :], self.TOTAL_P[:, 0:w]))
        link(nc.vector.tensor_tensor_scan(self.SUM[:, :], CST[:, RESET:RESET + w], self.TOTAL[:, :], 0.0, ALU.mult,
                                          ALU.add))
        link(nc.vector.tensor_tensor(self.SUM[:, :], self.SUM[:, :], self.TOTAL[:, :], ALU.subtract))
        link(nc.vector.tensor_tensor(rank, self.SUM[:, :], self.BEFORE_P[:, 0:w], ALU.add))

def select_phase(nc, CST, SC, MASKT):
    BITS = 30
    with Phase(nc, "select") as ph:
        shape = [P, E0, NT]
        FIRST, SECOND, EQ, REST, ROUTE, GE = (ph.sb(n, shape) for n in ("first", "second", "eq", "rest", "route", "ge"))
        BEST1, BEST2, INDEX, TOK = (ph.sb(n, [P, NT]) for n in ("best1", "best2", "index", "token"))
        CUR, CAND, BIT, TAKE = (ph.sb(n, [P, E0], I32) for n in ("threshold", "candidate", "bit", "take"))
        COUNT, NEED = ph.sb("count", [P, E0]), ph.sb("need", [P, E0])
        MASK = ph.sb("mask", shape, BF16)
        LARGE = ph.sb("large", shape, I32)
        IDB = ph.sb("ident_bf16", [P, P], BF16)
        TOTALS = ph.ps("totals")
        MT = [ph.ps(f"mask_t{k}", dt=BF16) for k in range(2)]
        ranks = Ranks(ph, E0)
        shifted, exps, counted, summed = (ph.sem(n) for n in ("shifted", "exps", "counts_ready", "counts_summed"))
        mask_ready, mt_ready, mt_copied, dchain = (ph.sem(n) for n in
                                                   ("mask_ready", "mask_t_ready", "mask_t_copied", "vector_chain"))
        block = ph.block()

        def per_token(a):
            return a[:, :].unsqueeze(1).to_broadcast(shape)

        def per_expert(a):
            return a.unsqueeze(2).to_broadcast(shape)

        @block.scalar
        def _(act):
            act.wait_ge(shifted, 1)
            nc.scalar.activation(ROUTE[:, :, :], ROUTE[:, :, :], ACT.Exp).then_inc(exps, 1)

        @block.tensor
        def _(pe):
            with pe.Fori(0, BITS + 1) as i:
                pe.wait_ge(counted, i + 1)
                nc.tensor.matmul(TOTALS[:, 0:E0], CST[:, ONES:ONES + P], COUNT[:, :], start=True, stop=True)\
                    .then_inc(summed, 1)
            ranks.count(nc, pe, CST, GE)
            pe.wait_ge(mask_ready, 1)
            for t in range(NT):
                if t % 4 == 0 and t >= 8:
                    pe.wait_ge(mt_copied, t // 4 - 1)
                mm = nc.tensor.transpose(MT[t // 4 % 2][0:E0, t % 4 * P:(t % 4 + 1) * P], MASK[:, :, t], IDB[:, :])
                if t % 4 == 3:
                    mm.then_inc(mt_ready, 1)

        @block.vector
        def _(dve):
            link = Chain(dve, dchain)
            link(nc.vector.tensor_copy(IDB[:, :], CST[:, IDENT:IDENT + P]))
            link(nc.vector.tensor_reduce(TOK[:, :], SC[:, :, :].rearrange("p e t -> p t e"), AX.X, ALU.max))
            nc.vector.tensor_tensor(ROUTE[:, :, :], SC[:, :, :], per_token(TOK), ALU.subtract).then_inc(shifted, 1)
            dve.wait_ge(exps, 1)
            link(nc.vector.tensor_reduce(TOK[:, :], ROUTE[:, :, :].rearrange("p e t -> p t e"), AX.X, ALU.add))
            link(nc.vector.reciprocal(TOK[:, :], TOK[:, :]))
            link(nc.vector.tensor_tensor(ROUTE[:, :, :], ROUTE[:, :, :], per_token(TOK), ALU.mult))
            top_two(nc, link, CST, ROUTE, E0, -4.0, (FIRST, SECOND, EQ, REST, BEST1, BEST2, INDEX))
            link(nc.vector.tensor_tensor(FIRST[:, :, :], FIRST[:, :, :], SECOND[:, :, :], ALU.add))
            link(nc.vector.tensor_tensor(ROUTE[:, :, :], ROUTE[:, :, :], FIRST[:, :, :], ALU.mult))
            link(nc.vector.tensor_scalar(REST[:, :, :], ROUTE[:, :, :], 1e-6, None, ALU.add))
            link(nc.vector.reciprocal(SECOND[:, :, :], REST[:, :, :]))
            link(nc.vector.tensor_scalar(LARGE[:, :, :], ROUTE[:, :, :], 2.0 ** -10, None, ALU.is_ge))
            link(nc.vector.tensor_tensor(GE[:, :, :], REST[:, :, :], ROUTE[:, :, :], ALU.subtract))
            link(nc.vector.tensor_tensor(GE[:, :, :], GE[:, :, :], SECOND[:, :, :], ALU.mult))
            link(nc.vector.tensor_scalar(GE[:, :, :], GE[:, :, :], -1.0, 1.0, ALU.mult, ALU.add))
            link(nc.vector.tensor_tensor(ROUTE[:, :, :], ROUTE[:, :, :], SECOND[:, :, :], ALU.mult))
            link(nc.vector.copy_predicated(ROUTE[:, :, :], LARGE[:, :, :], GE[:, :, :]))
            link(nc.vector.memset(CUR[:, :], 0))
            link(nc.vector.memset(BIT[:, :], 1 << (BITS - 1)))
            start, loop = link.n, 8
            with dve.Fori(0, BITS) as i:
                link.start(start + i * loop)
                link(nc.vector.tensor_tensor(CAND[:, :], CUR[:, :], BIT[:, :], ALU.bitwise_or))
                link(nc.vector.tensor_tensor(GE[:, :, :], ROUTE[:, :, :], per_expert(CAND[:, :].bitcast(F32)), ALU.is_ge))
                link(nc.vector.tensor_reduce(COUNT[:, :], GE[:, :, :], AX.X, ALU.add))
                dve.sem_inc(counted, 1)
                dve.wait_ge(summed, i + 1)
                link(nc.vector.tensor_scalar(NEED[:, :], TOTALS[:, 0:E0], KEEP0 - 0.5, -1.0, ALU.is_ge, ALU.mult))
                link(nc.vector.tensor_copy(TAKE[:, :], NEED[:, :]))
                link(nc.vector.tensor_tensor(TAKE[:, :], TAKE[:, :], BIT[:, :], ALU.bitwise_and))
                link(nc.vector.tensor_tensor(CUR[:, :], CUR[:, :], TAKE[:, :], ALU.bitwise_or))
                link(nc.vector.tensor_scalar(BIT[:, :], BIT[:, :], 1, None, ALU.logical_shift_right))
            link.start(start + BITS * loop)
            threshold = per_expert(CUR[:, :].bitcast(F32))
            link(nc.vector.tensor_tensor(FIRST[:, :, :], ROUTE[:, :, :], threshold, ALU.is_gt))
            link(nc.vector.tensor_reduce(COUNT[:, :], FIRST[:, :, :], AX.X, ALU.add))
            dve.sem_inc(counted, 1)
            dve.wait_ge(summed, BITS + 1)
            link(nc.vector.tensor_scalar(NEED[:, :], TOTALS[:, 0:E0], -1.0, float(KEEP0), ALU.mult, ALU.add))
            link(nc.vector.tensor_tensor(GE[:, :, :], ROUTE[:, :, :], threshold, ALU.is_equal))
            dve.sem_inc(ranks.mask_ready, 1)
            ranks.finish(nc, dve, link, CST, REST)
            link(nc.vector.tensor_tensor(REST[:, :, :], REST[:, :, :], per_expert(NEED[:, :]), ALU.is_lt))
            link(nc.vector.tensor_tensor(REST[:, :, :], REST[:, :, :], GE[:, :, :], ALU.mult))
            nc.vector.tensor_tensor(MASK[:, :, :], FIRST[:, :, :], REST[:, :, :], ALU.add).then_inc(mask_ready, 1)
            for n in range(NT // 4):
                dve.wait_ge(mt_ready, n + 1)
                nc.vector.tensor_copy(MASKT[:, n * CH:(n + 1) * CH], MT[n % 2][0:E0, :]).then_inc(mt_copied, 1)

def ffn0_phase(nc, w1, b1, w2, b2, gamma, beta, b_unify, CST, MASKT, X, XN, XNT):
    MF = F0 // P
    with Phase(nc, "ffn0") as ph:
        W1 = ph.sb("w1", [P, KC, F0])
        W2 = ph.sb("w2", [P, MF, C])
        B1 = ph.sb("b1", [P, MF])
        B2 = ph.sb("b2", [E0, C])
        ROWS = ph.sb("gamma_beta_bias", [P, 3, C])
        EXPB = ph.sb("expand_bf16", [E0, MF, P], BF16)
        MC = [ph.sb(f"mask_chunk{k}", [E0, CH]) for k in range(2)]
        MCB = [ph.sb(f"mask_chunk_bf16_{k}", [E0, CH], BF16) for k in range(2)]
        G = [ph.sb(f"gelu{k}", [P, CH]) for k in range(2)]
        GM = ph.sb("masked", [P, MF, CH])
        Z = ph.sb("z", [P, TC, C])
        STATS, MV = ph.sb("stats", [P, TC, 6]), ph.sb("mean_var", [P, TC, 2])
        VAR, STD, RSTD = (ph.sb(n, [P, TC]) for n in ("variance", "deviation", "rstd"))
        HP = [ph.ps(f"hidden{k}") for k in range(2)]
        MP = [ph.ps(f"mask{k}") for k in range(2)]
        OP = [ph.ps(f"out{k}") for k in range(2)]
        w_in, h_ready, g_done, m_ready, gm_done = (ph.sem(n) for n in
                                                   ("weights_in", "hidden_ready", "gelu_done", "mask_ready", "masked"))
        out_ready, out_used, exp_ready, mc_ready = (ph.sem(n) for n in
                                                    ("out_ready", "out_used", "expand_ready", "mask_chunk_ready"))
        var_ready, std_ready, stats_ready, dchain = (ph.sem(n) for n in
                                                     ("variance_ready", "deviation_ready", "stats_ready",
                                                      "vector_chain"))
        block = ph.block()

        @block.sync
        def _(sp):
            for k in range(KC):
                sp.dma_start(W1[:, k, :].rearrange("p (e f) -> p e f", e=E0),
                             w1[:, k * P:(k + 1) * P, :].rearrange("e p f -> p e f")).then_inc(w_in, 16)
            sp.dma_start(W2[:, :, :], w2.rearrange("(m a) f n -> (a f) m n", m=MF)).then_inc(w_in, 16)
            sp.dma_start(B1[:, :], b1.rearrange("(m a) f -> (a f) m", m=MF),
                         allow_slow_non_contiguous=True).then_inc(w_in, 16)
            sp.dma_start(B2[:, :], b2).then_inc(w_in, 16)
            for n, row in enumerate((gamma, beta, b_unify)):
                sp.dma_start(ROWS[:, n, :], row.rearrange("(a n) -> a n", a=1).to_broadcast([P, C])).then_inc(w_in, 16)
            sp.wait_ge(w_in, 8 * 16)

        @block.gpsimd
        def _(pool):
            with pool.Fori(0, NCH // 2) as i:
                for k in range(2):
                    n = 2 * i + k
                    pool.wait_ge(out_used, n + 1)
                    for chunk in (MC[k], MCB[k]):
                        nc.gpsimd.tensor_copy(chunk[:, :], MASKT[:, bass.ds(n * CH, CH)]).then_inc(mc_ready, 1)

        @block.tensor
        def _(pe):
            pe.wait_ge(w_in, 8 * 16)
            pe.wait_ge(exp_ready, 1)
            with pe.Fori(0, NCH // 2) as i:
                for k in range(2):
                    n = 2 * i + k
                    pe.wait_ge(mc_ready, 2 * (n + 1))
                    for m in range(MF):
                        pe.wait_ge(g_done, n * MF + m + 1)
                        for q in range(KC):
                            mm = nc.tensor.matmul(HP[m % 2][:, :], W1[:, q, m * P:(m + 1) * P],
                                                  XNT[:, q, bass.ds(n * CH, CH)], start=(q == 0), stop=(q == KC - 1))
                        mm.then_inc(h_ready, 1)
                        pe.wait_ge(gm_done, n * MF + m + 1)
                        nc.tensor.matmul(MP[m % 2][:, :], EXPB[:, m, :], MCB[k][:, :],
                                         start=True, stop=True).then_inc(m_ready, 1)
                    pe.wait_ge(gm_done, (n + 1) * MF + 2)
                    pe.wait_ge(out_used, n + 2)
                    for j in range(TC):
                        o = OP[j // 2][:, j % 2 * C:(j % 2 + 1) * C]
                        for m in range(MF):
                            nc.tensor.matmul(o, GM[:, m, j * P:(j + 1) * P], W2[:, m, :], start=(m == 0), stop=False)
                        mm = nc.tensor.matmul(o, MC[k][:, j * P:(j + 1) * P], B2[:, :], start=False, stop=True)
                        mm.then_inc(out_ready, 1)

        @block.scalar
        def _(act):
            act.sem_inc(g_done, 2)
            act.wait_ge(w_in, 8 * 16)
            with act.Fori(0, NCH // 2) as i:
                for k in range(2):
                    n = 2 * i + k
                    for m in range(MF):
                        act.wait_ge(h_ready, n * MF + m + 1)
                        act.wait_ge(gm_done, n * MF + m + 1)
                        nc.scalar.activation(G[m % 2][:, :], HP[m % 2][:, :], ACT.Gelu, bias=B1[:, m:m + 1])\
                            .then_inc(g_done, 1)
                    act.wait_ge(var_ready, n + 1)
                    nc.scalar.activation(STD[:, :], VAR[:, :], ACT.Sqrt).then_inc(std_ready, 1)

        @block.vector
        def _(dve):
            link = Chain(dve, dchain)
            dve.sem_inc(gm_done, 2)
            dve.sem_inc(out_used, 2)
            nc.vector.tensor_copy(EXPB[:, :, :].rearrange("p m q -> p (m q)"), CST[0:E0, EXPAND:EXPAND + MF * P])\
                .then_inc(exp_ready, 1)
            dve.wait_ge(w_in, 8 * 16)
            with dve.Fori(0, NCH // 2) as i:
                link.start(i * 18)
                for k in range(2):
                    n = 2 * i + k
                    for m in range(MF):
                        dve.wait_ge(g_done, n * MF + m + 3)
                        dve.wait_ge(m_ready, n * MF + m + 1)
                        nc.vector.tensor_tensor(GM[:, m, :], G[m % 2][:, :], MP[m % 2][:, :], ALU.mult)\
                            .then_inc(gm_done, 1)
                    for j in range(0, TC, 2):
                        dve.wait_ge(out_ready, n * TC + j + 2)
                        ins = nc.vector.tensor_tensor(Z[:, j:j + 2, :], OP[j // 2][:, :].rearrange("p (a c) -> p a c", a=2),
                                                      XN[:, bass.ds(n * TC + j, 2), :], ALU.add)
                    link(ins)
                    dve.sem_inc(out_used, 1)
                    for j in range(TC):
                        ins = nc.vector.bn_stats(STATS[:, j, :], Z[:, j, :])
                    link(ins)
                    dve.sem_inc(stats_ready, 1)
                    for j in range(TC):
                        ins = nc.vector.bn_aggr(MV[:, j, :], STATS[:, j, :])
                    link(ins)
                    link(nc.vector.tensor_scalar(VAR[:, :], MV[:, :, 1], LN_EPS, None, ALU.add))
                    dve.sem_inc(var_ready, 1)
                    dve.wait_ge(std_ready, n + 1)
                    link(nc.vector.reciprocal(RSTD[:, :], STD[:, :]))
                    for j in range(TC):
                        ins = nc.vector.tensor_scalar(Z[:, j, :], Z[:, j, :], MV[:, j, 0:1], RSTD[:, j:j + 1],
                                                      ALU.subtract, ALU.mult)
                    link(ins)
                    rows = [ROWS[:, r, :].unsqueeze(1).to_broadcast([P, TC, C]) for r in range(3)]
                    link(nc.vector.tensor_tensor(Z[:, :, :], Z[:, :, :], rows[0], ALU.mult))
                    link(nc.vector.tensor_tensor(Z[:, :, :], Z[:, :, :], rows[1], ALU.add))
                    link(nc.vector.tensor_tensor(Z[:, :, :], Z[:, :, :], rows[2], ALU.add))
                    xs = X[:, bass.ds(n * TC, TC), :]
                    nc.vector.tensor_tensor(xs, xs, Z[:, :, :], ALU.add)


def attention_phase(nc, q_scratch, k_scratch, V, ATT, CST, H=HEADS):
    NCH, NU, NA, NB = T // CH, T // CH, (CH // P) * (T // CH), 3
    R = 2 * NCH
    with Phase(nc, "attention") as ph:
        sb, ps, sem = ph.sb, ph.ps, ph.sem
        QOP = [sb(f"q_operand{b}", [P, T], F32R) for b in range(2)]
        KOP = [sb(f"k_operand{b}", [P, T], F32R) for b in range(2)]
        PR = sb("probs", [P, 8, CH])
        VH = [sb(f"v_head{b}", [P, NT, 32]) for b in range(2)]
        O4 = [sb(f"o_parts{b}", [P, CH]) for b in range(2)]
        MPART = [sb(f"max_parts{b}", [P, 4, 8]) for b in range(2)]
        M4 = sb("row_max", [P, 4])
        MSPLIT = sb("neg_max_split", [P, 4, 2], F32R)
        MROW = [sb(f"neg_max_row{b}", [2, CH], F32R) for b in range(2)]
        RDEN = sb("recip_den", [P, 4])

        ST = [ps(f"scores_t{b}", [P, CH]) for b in range(NB)]
        SA = [ps(f"scores_q{b}", [P, CH]) for b in range(NB)]
        OP = ps("o_psum", [P, CH])
        MISC = ps("misc_psum", [P, CH])

        loaded = [sem(f"operands_loaded{b}") for b in range(2)]
        ones_set = sem("ones_set")
        vh_ready = [sem(f"v_head_ready{b}") for b in range(2)]
        st_ready = sem("scores_ready")
        exp_done = sem("exp_done")
        sa_ready = sem("max_scores_ready")
        red_done = sem("max_part_done")
        pv_done = sem("pv_unit_done")
        o_copied = sem("o_copied")
        msplit = sem("neg_max_split_done")
        mt_ready = sem("neg_max_transposed")
        mrow_copied = sem("neg_max_row_copied")
        mrow_loaded = [sem(f"neg_max_row_loaded{b}") for b in range(2)]
        sel_ready = sem("o_summed")
        norm_done = sem("o_normalised")
        dchain = sem("vector_chain")
        o_init = sem("o_init")
        block = ph.block()
        NI, LOAD = H // 2, 7 * 16
        APART = 2 * R * NA

        def load_head(sp, h, b):
            q, k = QOP[b][:, :].bitcast(F32), KOP[b][:, :].bitcast(F32)
            for row, part_q, part_k in ((0, 1, 0), (D, 0, 0), (2 * D, 0, 1)):
                sp.dma_start(q[row:row + D, :], q_scratch[part_q, bass.ds(h * D, D), :]).then_inc(loaded[b], 16)
                sp.dma_start(k[row:row + D, :], k_scratch[part_k, bass.ds(h * D, D), :]).then_inc(loaded[b], 16)
            sp.dma_start(q[48:50, :], k[50:52, :]).then_inc(loaded[b], 16)

        def load_max_rows(sp, b, c, row, count):
            sp.wait_ge(mrow_copied, count)
            sp.dma_start(QOP[b][48:50, c * CH:(c + 1) * CH].bitcast(F32), MROW[row][:, :].bitcast(F32))\
                .then_inc(mrow_loaded[row], 16)

        @block.sync
        def _(sp):
            sp.wait_ge(ones_set, 10)
            load_head(sp, 0, 0)
            load_max_rows(sp, 0, 0, 0, 1)
            with sp.Fori(0, NI) as i:
                for r in range(R):
                    if r == 0:
                        sp.wait_ge(pv_done, i * (R * NU) + 2)
                        load_head(sp, 2 * i + 1, 1)
                    if r == NCH:
                        sp.wait_ge(pv_done, i * (R * NU) + NCH * NU + 2)
                        load_head(sp, (2 * i + 2) % H, 0)
                    n = r + 1
                    load_max_rows(sp, n // NCH % 2, n % NCH, n % 2, i * R + n + 1)
            for b in range(2):
                sp.wait_ge(loaded[b], LOAD * (NI + 1 - b))
                sp.wait_ge(mrow_loaded[b], 16 * (NI * NCH + 1 - b))

        @block.gpsimd
        def _(pool):
            fills = []
            for b in range(2):
                fills += [(KOP[b][:, :].bitcast(F32), 0.0), (QOP[b][:, :].bitcast(F32), 0.0),
                          (VH[b][:, :, D:32], 0.0)]
            for b in range(2):
                fills += [(KOP[b][32:50, :].bitcast(F32), 1.0), (VH[b][:, :, D:D + 1], 1.0)]
            for n, (where, value) in enumerate(fills):
                if n:
                    pool.wait_ge(ones_set, n)
                nc.gpsimd.memset(where, value).then_inc(ones_set, 1)

            def stage(h, b):
                nc.gpsimd.tensor_copy(VH[b][:, :, 0:D], V[:, :, bass.ds(h * D, D)]).then_inc(vh_ready[b], 1)

            pool.wait_ge(ones_set, 10)
            stage(0, 0)
            stage(1, 1)
            if NI > 1:
                with pool.Fori(0, NI - 1) as i:
                    pool.wait_ge(pv_done, i * (R * NU) + NCH * NU + 2)
                    stage(2 * i + 2, 0)
                    pool.wait_ge(pv_done, i * (R * NU) + R * NU + 2)
                    stage(2 * i + 3, 1)

        @block.tensor
        def _(pe):
            def max_scores(r, a, count):
                b, c, buffer = r // NCH, r % NCH, (r * NA + a) % NB
                qt, k = a // 8, a % 8
                pe.wait_ge(red_done, APART + count + (r * NA + a < (R * NA) % NB))
                nc.tensor.matmul(SA[buffer][:, :], QOP[b][:, c * CH + qt * P:c * CH + (qt + 1) * P],
                                 KOP[b][:, k * CH:(k + 1) * CH],
                                 start=True, stop=True).then_inc(sa_ready, 1)

            def score_tile(r, kt, count):
                b, c, buffer = r // NCH, r % NCH, (r * NT + kt) % NB
                pe.wait_ge(exp_done, count + (r * NT + kt < (R * NT) % NB))
                nc.tensor.matmul(ST[buffer][:, :], KOP[b][:, kt * P:(kt + 1) * P],
                                 QOP[b][:, c * CH:(c + 1) * CH], start=True, stop=True).then_inc(st_ready, 1)

            def pv_unit(b, u, exps):
                pe.wait_ge(exp_done, exps)
                for g in range(4):
                    kt = 4 * u + g
                    mm = nc.tensor.matmul(OP[32 * g:32 * g + 32, :], VH[b][:, kt, :], PR[:, kt % 8, :],
                                          start=(u == 0), stop=(u == NU - 1))
                mm.then_inc(pv_done, 1)

            def transpose_max(count, norms, rows_out):
                pe.wait_ge(msplit, count)
                pe.wait_ge(norm_done, norms)
                if rows_out is not None:
                    pe.wait_ge(mrow_copied, rows_out)
                for j in range(4):
                    mm = nc.tensor.transpose(MISC[0:2, j * P:(j + 1) * P], MSPLIT[:, j, :].bitcast(F32),
                                             CST[:, IDENT:IDENT + P])
                mm.then_inc(mt_ready, 1)

            def sum_parts(par, copies, rows_out):
                pe.wait_ge(o_copied, copies)
                pe.wait_ge(mrow_copied, rows_out)
                for j in range(4):
                    mm = nc.tensor.matmul(MISC[:, j * 32:j * 32 + D + 1], O4[par][:, j * P:(j + 1) * P],
                                          CST[:, SUMCOL:SUMCOL + D + 1], start=True, stop=True)
                mm.then_inc(sel_ready, 1)

            pe.wait_ge(loaded[0], LOAD)
            for a in range(NA):
                max_scores(0, a, a + 1)
            for a in range(NA):
                max_scores(1, a, NA + a + 1)
            transpose_max(1, 1, None)
            pe.wait_ge(mrow_loaded[0], 16)
            for kt in range(4):
                score_tile(0, kt, kt + 1)
            with pe.Fori(0, NI) as i:
                for r in range(R):
                    b = r // NCH
                    if r == NCH - 2:
                        pe.wait_ge(loaded[1], (i + 1) * LOAD)
                    if r == R - 2:
                        pe.wait_ge(loaded[0], (i + 2) * LOAD)
                    if r % NCH == 0:
                        pe.wait_ge(vh_ready[b], i + 1)
                    for u in range(NU):
                        for j in range(4):
                            a, n = 4 * u + j, r * NT + 4 * (u + 1) + j
                            max_scores((r + 2) % R, a, i * (R * NA) + (r + 2) * NA + a + 1)
                            if u == NU - 1 and j == 0:
                                pe.wait_ge(mrow_loaded[(r + 1) % 2], i * (16 * NCH) + 16 * ((r + 1) // 2 + 1))
                            if u < NU - 1:
                                score_tile(r, 4 * (u + 1) + j, i * (R * NT) + n + 1)
                            else:
                                score_tile((r + 1) % R, j, i * (R * NT) + n + 1)
                        if u == 0:
                            pe.wait_ge(o_copied, i * R + r + 1)
                        pv_unit(b, u, i * (R * NT) + r * NT + 4 * u + 4 + NB)
                        if u == 1:
                            transpose_max(i * R + r + 2, i * R + r + 1, i * R + r + 1)
                        if u == 4:
                            sum_parts(r % 2, i * R + r + 1, i * R + r + 2)
            sum_parts(0, NI * R + 1, NI * R + 1)

        @block.scalar
        def _(act):
            act.sem_inc(exp_done, NB)

            def copy_parts(par, units):
                act.wait_ge(pv_done, units)
                nc.scalar.copy(O4[par][:, :], OP[:, :]).then_inc(o_copied, 1)

            def copy_max_rows(row, count):
                act.wait_ge(mt_ready, count)
                nc.scalar.copy(MROW[row][:, :], MISC[0:2, :]).then_inc(mrow_copied, 1)

            copy_max_rows(0, 1)
            act.wait_ge(o_init, 1)
            with act.Fori(0, NI) as i:
                for r in range(R):
                    for kt in range(NT):
                        if kt % 4 == 0:
                            act.wait_ge(pv_done, i * (R * NU) + r * NU + kt // 4 + 1)
                        act.wait_ge(st_ready, i * (R * NT) + r * NT + kt + 1)
                        nc.scalar.activation(PR[:, kt % 8, :], ST[(r * NT + kt) % NB][:, :], ACT.Exp).then_inc(exp_done, 1)
                        if kt == 1:
                            copy_parts(r % 2, i * (R * NU) + r * NU + 2)
                        if kt == 10:
                            copy_max_rows((r + 1) % 2, i * R + r + 2)
            act.wait_ge(exp_done, NI * R * NT + NB)
            act.sem_inc(exp_done, 1)
            copy_parts(0, NI * R * NU + 2)

        @block.vector
        def _(dve):
            nc.vector.memset(OP[:, :], 1.0).then_inc(o_init, 1)
            dve.sem_inc(red_done, APART + NB)
            dve.sem_inc(pv_done, 2)
            dve.sem_inc(norm_done, 1)

            def reduce_block(par, a, buffer, count):
                dve.wait_ge(sa_ready, count)
                nc.vector.tensor_reduce(MPART[par][:, a // 8, a % 8:a % 8 + 1], SA[buffer][:, :], AX.X, ALU.max)\
                    .then_inc(red_done, 1)

            def split_max(par, parts, chain):
                dve.wait_ge(red_done, APART + parts)
                nc.vector.tensor_reduce(M4[:, :], MPART[par][:, :, :], AX.X, ALU.max).then_inc(dchain, 1)
                dve.wait_ge(dchain, chain + 1)
                nc.vector.tensor_scalar(MSPLIT[:, :, 0], M4[:, :], -1.0, None, ALU.mult).then_inc(dchain, 1)
                dve.wait_ge(dchain, chain + 2)
                nc.vector.scalar_tensor_tensor(MSPLIT[:, :, 1], M4[:, :], -1.0, MSPLIT[:, :, 0].bitcast(F32), ALU.mult,
                                               ALU.subtract).then_inc(msplit, 1)

            def normalise(slot, sums, chain):
                dve.wait_ge(sel_ready, sums)
                sums4 = MISC[:, 0:P].rearrange("p (j d) -> p j d", j=4)
                nc.vector.reciprocal(RDEN[:, :], sums4[:, :, D]).then_inc(dchain, 1)
                dve.wait_ge(dchain, chain + 1)
                nc.vector.tensor_tensor(ATT[:, slot, :].rearrange("p (j d) -> p j d", d=D), sums4[:, :, 0:D],
                                        RDEN[:, :].unsqueeze(2).to_broadcast([P, 4, D]), ALU.mult)\
                    .then_inc(norm_done, 1)

            for a in range(NA):
                reduce_block(0, a, a % NB, a + 1)
            split_max(0, NA + NB, 0)
            for a in range(NA):
                reduce_block(1, a, (NA + a) % NB, NA + a + 1)
            with dve.Fori(0, NI) as i:
                for r in range(R):
                    dve.wait_ge(mt_ready, i * R + r + 1)
                    split_max((r + 1) % 2, i * (R * NA) + (r + 2) * NA + NB, i * (R * 3) + r * 3 + 2)
                    for a in range(NA):
                        reduce_block(r % 2, a, ((r + 2) % R * NA + a) % NB, i * (R * NA) + (r + 2) * NA + a + 1)
                        if a == 22:
                            normalise(i * R + r, i * R + r + 1, i * (R * 3) + r * 3 + 4)
            normalise(NI * R, NI * R + 1, NI * R * 3 + 2)


def unify_phase(nc, w_unify, norm_w, CST, ATT, X, XN1, XT1, YT, DISP):
    with Phase(nc, "unify") as ph:
        WU = ph.sb("w_unify", [P, KC, C])
        NW = ph.sb("norm_w", [P, KC])
        AC = ph.sb("attention_chunk", [P, TC, C])
        AT = ph.sb("attention_t", [P, KC, CH])
        XG = ph.sb("xn_chunk", [P, TC, C])
        YG = ph.sb("y_chunk", [P, TC, C])
        STATS, MV = ph.sb("stats", [P, TC, 6]), ph.sb("mean_var", [P, TC, 2])
        VAR, STD, RSTD, MS, RMS, RRMS = (ph.sb(n, [P, TC]) for n in
                                         ("variance", "deviation", "rstd", "mean_square", "rms", "recip_rms"))
        ZERO = ph.sb("zero", [P, 1024])
        TP = [ph.ps(f"transposed{k}") for k in range(KC)]
        UP = [ph.ps(f"unified{k}") for k in range(2)]
        NP = [ph.ps(f"norm_transposed{k}") for k in range(2 * KC)]
        w_in, cleared, zero_set = ph.sem("weights_in"), ph.sem("rows_cleared"), ph.sem("zero_set")
        ac_ready, t_ready, at_ready = ph.sem("chunk_ready"), ph.sem("transposed_ready"), ph.sem("attention_t_ready")
        u_ready, var_ready, std_ready = ph.sem("unified_ready"), ph.sem("variance_ready"), ph.sem("deviation_ready")
        ms_ready, rms_ready, stats_ready = ph.sem("mean_square_ready"), ph.sem("rms_ready"), ph.sem("stats_ready")
        xg_ready, yg_ready, n_ready = ph.sem("xn_ready"), ph.sem("y_ready"), ph.sem("norm_transposed_ready")
        n_copied, xn_kept, dchain = ph.sem("norm_copied"), ph.sem("xn_kept"), ph.sem("vector_chain")
        block = ph.block()

        @block.sync
        def _(sp):
            sp.dma_start(WU[:, :, :], w_unify.rearrange("(k p) n -> p k n", p=P)).then_inc(w_in, 16)
            sp.dma_start(NW[:, :], norm_w.rearrange("(k p) -> p k", p=P), allow_slow_non_contiguous=True)\
                .then_inc(w_in, 16)
            sp.wait_ge(zero_set, 2)
            rows = DISP.rearrange("(n p r) c -> n p (r c)", p=P, r=4)
            for n in range(rows.shape[0]):
                sp.dma_start(rows[n], ZERO[:, :]).then_inc(cleared, 16)
            sp.wait_ge(cleared, 16 * rows.shape[0])

        @block.gpsimd
        def _(pool):
            nc.gpsimd.memset(ZERO[:, :], 0.0).then_inc(zero_set, 1)
            pool.wait_ge(zero_set, 1)
            nc.gpsimd.memset(YT[:, :, 0:1], 0.0)
            pool.wait_ge(w_in, 32)
            nc.gpsimd.memset(YT[:, :, T + 1:T + 2], 0.0).then_inc(zero_set, 1)
            with pool.Fori(0, NCH) as n:
                pool.wait_ge(at_ready, (n + 1) * KC)
                for j in range(TC):
                    ins = nc.gpsimd.tensor_copy(
                        AC[:, j, :].rearrange("p (h d) -> p h d", d=D),
                        ATT[:, 1:, :].rearrange("p (h c) x -> p h (c x)", c=NCH)[:, :, bass.ds(n * (TC * D) + j * D, D)])
                    ins.then_inc(ac_ready, 1)
                pool.wait_ge(xg_ready, n + 1)
                nc.gpsimd.tensor_copy(XN1[:, bass.ds(n * TC, TC), :], XG[:, :, :]).then_inc(xn_kept, 1)

        @block.tensor
        def _(pe):
            ident = CST[:, IDENT:IDENT + P]
            pe.wait_ge(w_in, 32)
            with pe.Fori(0, NCH) as n:
                pe.wait_ge(ac_ready, (n + 1) * TC)
                for m in range(KC):
                    for j in range(TC):
                        mm = nc.tensor.transpose(TP[m][:, j * P:(j + 1) * P], AC[:, j, m * P:(m + 1) * P], ident)
                    mm.then_inc(t_ready, 1)
                pe.wait_ge(at_ready, (n + 2) * KC)
                for j in range(TC):
                    for q in range(KC):
                        mm = nc.tensor.matmul(UP[j // 2][:, j % 2 * C:(j % 2 + 1) * C], AT[:, q, j * P:(j + 1) * P],
                                              WU[:, q, :], start=(q == 0), stop=(q == KC - 1))
                mm.then_inc(u_ready, 1)
                pe.wait_ge(n_copied, (n + 1) * 2 * KC)
                for g, (src, ready) in enumerate(((XG, xg_ready), (YG, yg_ready))):
                    pe.wait_ge(ready, n + 1)
                    for m in range(KC):
                        for j in range(TC):
                            mm = nc.tensor.transpose(NP[g * KC + m][:, j * P:(j + 1) * P],
                                                     src[:, j, m * P:(m + 1) * P], ident)
                        mm.then_inc(n_ready, 1)

        @block.scalar
        def _(act):
            act.sem_inc(at_ready, KC)
            act.sem_inc(xn_kept, 1)
            act.sem_inc(n_copied, 2 * KC)
            act.wait_ge(w_in, 32)
            with act.Fori(0, NCH) as n:
                for m in range(KC):
                    act.wait_ge(t_ready, n * KC + m + 1)
                    nc.scalar.copy(AT[:, m, :], TP[m][:, :]).then_inc(at_ready, 1)
                act.wait_ge(var_ready, n + 1)
                nc.scalar.activation(STD[:, :], VAR[:, :], ACT.Sqrt).then_inc(std_ready, 1)
                act.wait_ge(ms_ready, n + 1)
                nc.scalar.activation(RMS[:, :], MS[:, :], ACT.Sqrt).then_inc(rms_ready, 1)
                for m in range(KC):
                    act.wait_ge(n_ready, n * 2 * KC + m + 1)
                    nc.scalar.copy(XT1[:, m, bass.ds(n * CH, CH)], NP[m][:, :]).then_inc(n_copied, 1)
                for m in range(KC):
                    act.wait_ge(n_ready, n * 2 * KC + KC + m + 1)
                    nc.scalar.activation(YT[:, m, bass.ds(n * CH + 1, CH)], NP[KC + m][:, :], ACT.Copy,
                                         scale=NW[:, m:m + 1]).then_inc(n_copied, 1)

        @block.vector
        def _(dve):
            link = Chain(dve, dchain)
            with dve.Fori(0, NCH) as n:
                link.start(n * 11)
                xs = X[:, bass.ds(n * TC, TC), :]
                dve.wait_ge(u_ready, n + 1)
                for h in range(2):
                    two = X[:, bass.ds(n * TC + 2 * h, 2), :]
                    ins = nc.vector.tensor_tensor(two, UP[h][:, :].rearrange("p (a c) -> p a c", a=2), two, ALU.add)
                link(ins)
                dve.sem_inc(stats_ready, 1)
                for j in range(TC):
                    ins = nc.vector.bn_stats(STATS[:, j, :], X[:, bass.ds(n * TC + j, 1), :].rearrange("p a c -> p (a c)"))
                link(ins)
                dve.sem_inc(stats_ready, 1)
                for j in range(TC):
                    ins = nc.vector.bn_aggr(MV[:, j, :], STATS[:, j, :])
                link(ins)
                link(nc.vector.tensor_scalar(VAR[:, :], MV[:, :, 1], LN_EPS, None, ALU.add))
                dve.sem_inc(var_ready, 1)
                dve.wait_ge(std_ready, n + 1)
                link(nc.vector.reciprocal(RSTD[:, :], STD[:, :]))
                dve.wait_ge(n_copied, (n + 1) * 2 * KC)
                dve.wait_ge(xn_kept, n + 1)
                for j in range(TC):
                    ins = nc.vector.tensor_scalar(XG[:, j, :], X[:, bass.ds(n * TC + j, 1), :].rearrange("p a c -> p (a c)"),
                                                  MV[:, j, 0:1], RSTD[:, j:j + 1], ALU.subtract, ALU.mult)
                link(ins)
                dve.sem_inc(xg_ready, 1)
                for j in range(TC):
                    ins = nc.vector.tensor_tensor(YG[:, j, :], XG[:, j, :], XG[:, j, :], ALU.mult)
                link(ins)
                link(nc.vector.tensor_reduce(MS[:, :], YG[:, :, :], AX.X, ALU.add))
                link(nc.vector.tensor_scalar(MS[:, :], MS[:, :], 1.0 / C, 1e-6, ALU.mult, ALU.add))
                dve.sem_inc(ms_ready, 1)
                dve.wait_ge(rms_ready, n + 1)
                link(nc.vector.reciprocal(RRMS[:, :], RMS[:, :]))
                for j in range(TC):
                    ins = nc.vector.tensor_scalar(YG[:, j, :], XG[:, j, :], RRMS[:, j:j + 1], None, ALU.mult)
                link(ins)
                dve.sem_inc(yg_ready, 1)


def router_phase(nc, rw1, rb1, rw2, rb2, conv_w, conv_b, a, b, CST, XT1, YT, X2T, LG):
    with Phase(nc, "router") as ph:
        W1 = ph.sb("w1", [P, KC, HID])
        W2 = ph.sb("w2", [P, MH, E1])
        B1 = ph.sb("b1", [P, MH])
        B2 = ph.sb("b2", [P, E1])
        CW = ph.sb("conv_w", [P, KC, 3])
        CB, AV, BV, S = (ph.sb(n, [P, KC]) for n in ("conv_b", "a", "b", "decay"))
        RH = ph.sb("hidden", [P, MH, CH])
        HP = [ph.ps(f"hidden{k}") for k in range(3)]
        LP = [ph.ps(f"logits{k}") for k in range(2)]
        w_in, h_ready, r_done, l_ready, l_copied = (ph.sem(n) for n in
                                                    ("weights_in", "hidden_ready", "relu_done", "logits_ready",
                                                     "logits_copied"))
        s_ready, dchain = ph.sem("decay_ready"), ph.sem("vector_chain")
        block = ph.block()
        NW_IN = 8 * 16

        @block.sync
        def _(sp):
            sp.dma_start(W1[:, :, :], rw1.rearrange("(k p) n -> p k n", p=P)).then_inc(w_in, 16)
            sp.dma_start(W2[:, :, :], rw2.rearrange("(m p) e -> p m e", p=P)).then_inc(w_in, 16)
            sp.dma_start(B1[:, :], rb1.rearrange("(m p) -> p m", p=P), allow_slow_non_contiguous=True).then_inc(w_in, 16)
            sp.dma_start(B2[:, :], rb2.rearrange("(o e) -> o e", o=1).to_broadcast([P, E1])).then_inc(w_in, 16)
            sp.dma_start(CW[:, :, :], conv_w.rearrange("(k p) o w -> p k (o w)", p=P)).then_inc(w_in, 16)
            for dst, src in ((CB, conv_b), (AV, a), (BV, b)):
                sp.dma_start(dst[:, :], src.rearrange("(k p) -> p k", p=P), allow_slow_non_contiguous=True)\
                    .then_inc(w_in, 16)

        @block.tensor
        def _(pe):
            pe.wait_ge(w_in, NW_IN)
            with pe.Fori(0, NCH) as n:
                for m in range(MH):
                    pe.wait_ge(r_done, n * MH + m + 1 + (m < MH % 3))
                    for q in range(KC):
                        mm = nc.tensor.matmul(HP[m % 3][:, :], W1[:, q, m * P:(m + 1) * P],
                                              XT1[:, q, bass.ds(n * CH, CH)], start=(q == 0), stop=(q == KC - 1))
                    mm.then_inc(h_ready, 1)
                pe.wait_ge(r_done, (n + 1) * MH + 3)
                pe.wait_ge(l_copied, n + 1)
                for j in range(TC):
                    for m in range(MH):
                        mm = nc.tensor.matmul(LP[0][:, j * E1:(j + 1) * E1], RH[:, m, j * P:(j + 1) * P], W2[:, m, :],
                                              start=(m == 0), stop=(m == MH - 1))
                mm.then_inc(l_ready, 1)

        @block.scalar
        def _(act):
            act.sem_inc(r_done, 3)
            act.wait_ge(w_in, NW_IN)
            nc.scalar.activation(S[:, :], AV[:, :], ACT.Tanh).then_inc(s_ready, 1)
            with act.Fori(0, NCH) as n:
                for m in range(MH):
                    act.wait_ge(h_ready, n * MH + m + 1)
                    act.wait_ge(l_copied, n + 1)
                    nc.scalar.activation(RH[:, m, :], HP[m % 3][:, :], ACT.Relu, bias=B1[:, m:m + 1]).then_inc(r_done, 1)
                act.wait_ge(l_ready, n + 1)
                nc.scalar.copy(LG[:, :, bass.ds(n * TC, TC)].rearrange("p e t -> p t e"),
                               LP[0][:, 0:TC * E1].rearrange("p (t e) -> p t e", e=E1)).then_inc(l_copied, 1)

        @block.vector
        def _(dve):
            dve.sem_inc(l_copied, 1)
            link = Chain(dve, dchain)
            dve.wait_ge(w_in, NW_IN)
            dve.wait_ge(s_ready, 1)
            for k in range(KC):
                x2, y = X2T[:, k, :], YT[:, k, :]
                link(nc.vector.tensor_scalar(x2, y[:, 1:T + 1], BV[:, k:k + 1], None, ALU.mult))
                link(nc.vector.tensor_tensor_scan(x2, S[:, k:k + 1].to_broadcast([P, T]), x2, 0.0, ALU.mult, ALU.add))
                for w in range(3):
                    link(nc.vector.scalar_tensor_tensor(x2, y[:, w:w + T], CW[:, k, w:w + 1], x2, ALU.mult, ALU.add))
                link(nc.vector.scalar_tensor_tensor(x2, XT1[:, k, :], CB[:, k:k + 1], x2, ALU.add, ALU.add))
            dve.wait_ge(l_copied, NCH + 1)
            link(nc.vector.tensor_tensor(LG[:, :, :], LG[:, :, :], B2[:, :].unsqueeze(2).to_broadcast([P, E1, NT]),
                                         ALU.add))


def dispatch_phase(nc, CST, LG, SLOTS, WEIGHTS):
    with Phase(nc, "dispatch") as ph:
        shape = [P, E1, NT]
        FIRST, SECOND, EQ, REST, MASK, RANK = (ph.sb(n, shape) for n in ("first", "second", "eq", "rest", "mask", "rank"))
        BEST1, BEST2, INDEX, POS, BASE, FULL, PROB = (ph.sb(n, [P, NT]) for n in
                                                      ("best1", "best2", "index", "pos", "base", "full", "prob"))
        ranks = Ranks(ph, E1)
        diff_ready, exp_ready, dchain = ph.sem("difference_ready"), ph.sem("exp_ready"), ph.sem("vector_chain")
        block = ph.block()
        iota = CST[:, IOTA:IOTA + E1 * NT].rearrange("p (e t) -> p e t", t=NT)

        @block.scalar
        def _(act):
            act.wait_ge(diff_ready, 1)
            nc.scalar.activation(PROB[:, :], PROB[:, :], ACT.Exp).then_inc(exp_ready, 1)

        @block.tensor
        def _(pe):
            ranks.count(nc, pe, CST, MASK)

        @block.vector
        def _(dve):
            link = Chain(dve, dchain)
            top_two(nc, link, CST, LG, E1, -3.0e38, (FIRST, SECOND, EQ, REST, BEST1, BEST2, INDEX))
            link(nc.vector.tensor_tensor(PROB[:, :], BEST2[:, :], BEST1[:, :], ALU.subtract))
            dve.sem_inc(diff_ready, 1)
            link(nc.vector.tensor_tensor(MASK[:, :, :], FIRST[:, :, :], SECOND[:, :, :], ALU.add))
            dve.sem_inc(ranks.mask_ready, 1)
            ranks.finish(nc, dve, link, CST, RANK)
            dve.wait_ge(exp_ready, 1)
            link(nc.vector.tensor_scalar(WEIGHTS[:, 0, :], PROB[:, :], 1.0, None, ALU.add))
            link(nc.vector.reciprocal(WEIGHTS[:, 0, :], WEIGHTS[:, 0, :]))
            link(nc.vector.tensor_tensor(WEIGHTS[:, 1, :], PROB[:, :], WEIGHTS[:, 0, :], ALU.mult))
            for k, hot in enumerate((FIRST, SECOND)):
                for dst, what in ((POS, RANK[:, :, :]), (BASE, iota)):
                    link(nc.vector.tensor_tensor(EQ[:, :, :], hot[:, :, :], what, ALU.mult))
                    link(nc.vector.tensor_reduce(dst[:, :], EQ[:, :, :].rearrange("p e t -> p t e"), AX.X, ALU.add))
                link(nc.vector.tensor_scalar(BASE[:, :], BASE[:, :], float(CAP), None, ALU.mult))
                link(nc.vector.tensor_scalar(FULL[:, :], POS[:, :], CAP - 0.5, float(1 << 20), ALU.is_ge, ALU.mult))
                link(nc.vector.tensor_tensor(INDEX[:, :], BASE[:, :], POS[:, :], ALU.add))
                link(nc.vector.tensor_tensor(INDEX[:, :], INDEX[:, :], FULL[:, :], ALU.add))
                link(nc.vector.tensor_copy(SLOTS[:, k, :], INDEX[:, :]))
                link(nc.vector.tensor_scalar(INDEX[:, :], POS[:, :], CAP - 1.0, None, ALU.min))
                link(nc.vector.tensor_tensor(INDEX[:, :], INDEX[:, :], BASE[:, :], ALU.add))
                link(nc.vector.tensor_copy(SLOTS[:, 2 + k, :], INDEX[:, :]))
                link(nc.vector.tensor_scalar(FULL[:, :], POS[:, :], CAP - 0.5, None, ALU.is_lt))
                link(nc.vector.tensor_tensor(WEIGHTS[:, k, :], WEIGHTS[:, k, :], FULL[:, :], ALU.mult))


def z_phase(nc, mlp_norm_w, CST, X2T, ZT):
    with Phase(nc, "z") as ph:
        NW = ph.sb("norm_w", [P, KC])
        EPS = ph.sb("eps", [P, 1])
        SQ = [ph.sb(f"squares{k}", [P, KC, CH]) for k in range(2)]
        RMS = [ph.sb(f"rms{k}", [P, CH]) for k in range(2)]
        SP_ = [ph.ps(f"sums{k}") for k in range(2)]
        eps_set = ph.sem("eps_set")
        w_in, sq_ready, s_ready, rms_ready, z_done, dchain = (ph.sem(n) for n in
                                                              ("weights_in", "squares_ready", "sums_ready", "rms_ready",
                                                               "z_done", "vector_chain"))
        block = ph.block()

        @block.sync
        def _(sp):
            sp.dma_start(NW[:, :], mlp_norm_w.rearrange("(k p) -> p k", p=P), allow_slow_non_contiguous=True)\
                .then_inc(w_in, 16)
            sp.wait_ge(w_in, 16)

        @block.gpsimd
        def _(pool):
            nc.gpsimd.memset(EPS[:, :], 1e-6).then_inc(eps_set, 1)
            with pool.Fori(0, NCH // 2) as i:
                for k in range(2):
                    pool.wait_ge(z_done, 2 * i + k + 1)
                    xs = X2T[:, :, bass.ds((2 * i + k) * CH, CH)]
                    nc.gpsimd.tensor_tensor(SQ[k][:, :, :], xs, xs, ALU.mult).then_inc(sq_ready, 1)

        @block.tensor
        def _(pe):
            with pe.Fori(0, NCH // 2) as i:
                for k in range(2):
                    pe.wait_ge(sq_ready, 2 * i + k + 1)
                    for q in range(KC):
                        mm = nc.tensor.matmul(SP_[k][:, :], CST[:, ONES:ONES + P], SQ[k][:, q, :], start=(q == 0),
                                              stop=(q == KC - 1))
                    mm.then_inc(s_ready, 1)

        @block.scalar
        def _(act):
            act.wait_ge(eps_set, 1)
            with act.Fori(0, NCH // 2) as i:
                for k in range(2):
                    act.wait_ge(s_ready, 2 * i + k + 1)
                    nc.scalar.activation(RMS[k][:, :], SP_[k][:, :], ACT.Sqrt, bias=EPS[:, :], scale=1.0 / C)\
                        .then_inc(rms_ready, 1)

        @block.vector
        def _(dve):
            link = Chain(dve, dchain)
            dve.sem_inc(z_done, 2)
            dve.wait_ge(w_in, 16)
            with dve.Fori(0, NCH // 2) as i:
                link.start(i * 4)
                for k in range(2):
                    dve.wait_ge(rms_ready, 2 * i + k + 1)
                    link(nc.vector.reciprocal(RMS[k][:, :], RMS[k][:, :]))
                    for q in range(KC):
                        ins = nc.vector.scalar_tensor_tensor(ZT[:, q, bass.ds((2 * i + k) * CH, CH)],
                                                             X2T[:, q, bass.ds((2 * i + k) * CH, CH)], NW[:, q:q + 1],
                                                             RMS[k][:, :], ALU.mult, ALU.mult)
                    link(ins)
                    dve.sem_inc(z_done, 1)


def mlp_phase(nc, w_gate, b_gate, w_up, b_up, w_down, b_down, CST, ZT, X2T, X, XN1, SLOTS, DISP):
    with Phase(nc, "mlp") as ph:
        WG, WU = ph.sb("w_gate", [P, KC, HID]), ph.sb("w_up", [P, KC, HID])
        WD = ph.sb("w_down", [P, MH, C])
        BG, BU = ph.sb("b_gate", [P, MH]), ph.sb("b_up", [P, MH])
        BD = ph.sb("b_down", [P, C])
        XC = [ph.sb(f"x2_chunk{k}", [P, KC, CH]) for k in range(2)]
        G = [ph.sb(f"silu{k}", [P, CH]) for k in range(2)]
        H = ph.sb("hidden", [P, MH, CH])
        GP = [ph.ps(f"gate{k}") for k in range(2)]
        UP = [ph.ps(f"up{k}") for k in range(2)]
        OP = [ph.ps(f"out{k}") for k in range(2)]
        w_in, xc_in = ph.sem("weights_in"), [ph.sem(f"x2_in{k}") for k in range(2)]
        g_ready, u_ready, s_done, h_done, o_ready, o_used = (ph.sem(n) for n in
                                                             ("gate_ready", "up_ready", "silu_done", "hidden_done",
                                                              "out_ready", "out_used"))
        scattered, dchain = ph.sem("rows_written"), ph.sem("vector_chain")
        block = ph.block()
        NW_IN = 6 * 16

        @block.sync
        def _(sp):
            sp.dma_start(WG[:, :, :], w_gate.rearrange("(k p) n -> p k n", p=P)).then_inc(w_in, 16)
            sp.dma_start(WU[:, :, :], w_up.rearrange("(k p) n -> p k n", p=P)).then_inc(w_in, 16)
            sp.dma_start(WD[:, :, :], w_down.rearrange("(m p) n -> p m n", p=P)).then_inc(w_in, 16)
            for dst, src in ((BG, b_gate), (BU, b_up)):
                sp.dma_start(dst[:, :], src.rearrange("(m p) -> p m", p=P), allow_slow_non_contiguous=True)\
                    .then_inc(w_in, 16)
            sp.dma_start(BD[:, :], b_down.rearrange("(a n) -> a n", a=1).to_broadcast([P, C])).then_inc(w_in, 16)
            with sp.Fori(0, NCH // 2) as i:
                for k in range(2):
                    sp.wait_ge(o_used, 2 * i + k + 1)
                    sp.dma_start(XC[k][:, :, :], X2T[:, :, bass.ds((2 * i + k) * CH, CH)]).then_inc(xc_in[k], 16)

        @block.gpsimd
        def _(pool):
            for t in range(NT):
                for k in range(2):
                    pool.indirect_dma_start(DISP, bass.IndirectOffsetOnAxis(ap=SLOTS[:, k, t:t + 1], axis=0),
                                            XN1[:, t, :], None, bounds_check=E1 * CAP - 1, oob_is_err=False)\
                        .then_inc(scattered, 16)
            pool.wait_ge(scattered, 2 * NT * 16)

        @block.tensor
        def _(pe):
            pe.wait_ge(w_in, NW_IN)
            with pe.Fori(0, NCH // 2) as i:
                for k in range(2):
                    n = 2 * i + k
                    for m in range(MH):
                        pe.wait_ge(h_done, n * MH + m + 1)
                        for bank, w, ready in ((GP, WG, g_ready), (UP, WU, u_ready)):
                            for q in range(KC):
                                mm = nc.tensor.matmul(bank[m % 2][:, :], w[:, q, m * P:(m + 1) * P],
                                                      ZT[:, q, bass.ds(n * CH, CH)], start=(q == 0), stop=(q == KC - 1))
                            mm.then_inc(ready, 1)
                    pe.wait_ge(h_done, (n + 1) * MH + 2)
                    pe.wait_ge(o_used, n + 2)
                    pe.wait_ge(xc_in[k], (i + 1) * 16)
                    for j in range(TC):
                        o = OP[j // 2][:, j % 2 * C:(j % 2 + 1) * C]
                        for m in range(MH):
                            nc.tensor.matmul(o, H[:, m, j * P:(j + 1) * P], WD[:, m, :], start=(m == 0),
                                             stop=(m == MH - 1))
                        for q in range(KC):
                            mm = nc.tensor.matmul(o[:, q * P:(q + 1) * P], XC[k][:, q, j * P:(j + 1) * P],
                                                  CST[:, IDENT:IDENT + P], start=False, stop=True,
                                                  skip_group_check=True)
                        mm.then_inc(o_ready, 1)

        @block.scalar
        def _(act):
            act.wait_ge(w_in, NW_IN)
            with act.Fori(0, NCH // 2) as i:
                for k in range(2):
                    n = 2 * i + k
                    for m in range(MH):
                        act.wait_ge(g_ready, n * MH + m + 1)
                        act.wait_ge(h_done, n * MH + m + 1)
                        nc.scalar.activation(G[m % 2][:, :], GP[m % 2][:, :], ACT.Silu, bias=BG[:, m:m + 1])\
                            .then_inc(s_done, 1)

        @block.vector
        def _(dve):
            link = Chain(dve, dchain)
            dve.sem_inc(h_done, 2)
            dve.sem_inc(o_used, 2)
            dve.wait_ge(w_in, NW_IN)
            with dve.Fori(0, NCH // 2) as i:
                link.start(i * 4)
                for k in range(2):
                    n = 2 * i + k
                    for m in range(MH):
                        dve.wait_ge(s_done, n * MH + m + 1)
                        dve.wait_ge(u_ready, n * MH + m + 1)
                        nc.vector.scalar_tensor_tensor(H[:, m, :], UP[m % 2][:, :], BU[:, m:m + 1], G[m % 2][:, :],
                                                       ALU.add, ALU.mult).then_inc(h_done, 1)
                    for h in range(2):
                        dve.wait_ge(o_ready, n * TC + 2 * h + 2)
                        two = X[:, bass.ds(n * TC + 2 * h, 2), :]
                        ins = nc.vector.tensor_tensor(two, OP[h][:, :].rearrange("p (a c) -> p a c", a=2), two, ALU.add)
                    link(ins)
                    dve.sem_inc(o_used, 1)
                    xs = X[:, bass.ds(n * TC, TC), :]
                    link(nc.vector.tensor_tensor(xs, xs, BD[:, :].unsqueeze(1).to_broadcast([P, TC, C]), ALU.add))


def expert_phase(nc, ew1, eb1, ew2, eb2, CST, DISP, EOUT):
    NS = CAP // P
    with Phase(nc, "experts") as ph:
        W1 = [ph.sb(f"w1_{k}", [P, KC, HID]) for k in range(2)]
        W2 = [ph.sb(f"w2_{k}", [P, MH, C]) for k in range(2)]
        B1 = [ph.sb(f"b1_{k}", [P, MH]) for k in range(2)]
        B2 = [ph.sb(f"b2_{k}", [P, C]) for k in range(2)]
        R = [ph.sb(f"rows{k}", [P, NS, C]) for k in range(2)]
        RT = ph.sb("rows_t", [P, KC, CH])
        H = ph.sb("hidden", [P, MH, CH])
        O = [ph.sb(f"out{k}", [P, TC, C]) for k in range(2)]
        TP = [ph.ps(f"transposed{k}") for k in range(KC)]
        HP = [ph.ps(f"hidden{k}") for k in range(2)]
        OP = [ph.ps(f"out{k}") for k in range(2)]
        loaded = [ph.sem(f"expert_in{k}") for k in range(2)]
        stored = [ph.sem(f"out_stored{k}") for k in range(2)]
        t_ready, rt_ready, h_ready, r_done, o_ready, o_copied = (ph.sem(n) for n in
                                                                 ("transposed_ready", "rows_t_ready", "hidden_ready",
                                                                  "relu_done", "out_ready", "out_copied"))
        block = ph.block()

        @block.sync
        def _(sp):
            rows = EOUT.rearrange("(n p) c -> p n c", p=P)

            def load(e, k):
                sp.dma_start(W1[k][:, :, :], ew1.rearrange("e (k p) n -> p e k n", p=P)[:, bass.ds(e, 1)]
                             .rearrange("p e k n -> p (e k) n")).then_inc(loaded[k], 16)
                sp.dma_start(W2[k][:, :, :], ew2.rearrange("e (m p) n -> p e m n", p=P)[:, bass.ds(e, 1)]
                             .rearrange("p e m n -> p (e m) n")).then_inc(loaded[k], 16)
                sp.dma_start(B1[k][:, :], eb1.rearrange("e (m p) -> p e m", p=P)[:, bass.ds(e, 1)]
                             .rearrange("p e m -> p (e m)"), allow_slow_non_contiguous=True).then_inc(loaded[k], 16)
                sp.dma_start(B2[k][:, :], eb2[bass.ds(e, 1), :].to_broadcast([P, C])).then_inc(loaded[k], 16)
                sp.dma_start(R[k][:, :, :], DISP.rearrange("(n p) c -> p n c", p=P)[:, bass.ds(e * NS, NS), :])\
                    .then_inc(loaded[k], 16)

            def store(e):
                for h in range(2):
                    sp.wait_ge(o_copied, e * 4 + 2 * h + 12)
                    sp.dma_start(rows[:, bass.ds(e * NS + h * TC, TC), :], O[h][:, :, :]).then_inc(stored[h], 16)

            for k in range(2):
                load(k, k)
            with sp.Fori(0, E1 // 2 - 1) as i:
                for k in range(2):
                    store(2 * i + k)
                    load(2 * i + k + 2, k)
            for k in range(2):
                store(E1 - 2 + k)
            for h in range(2):
                sp.wait_ge(stored[h], (E1 + 1) * 16)

        @block.tensor
        def _(pe):
            ident = CST[:, IDENT:IDENT + P]
            with pe.Fori(0, E1 // 2) as i:
                for k in range(2):
                    pe.wait_ge(loaded[k], (i + 1) * 80)
                    for h in range(2):
                        g = 4 * i + 2 * k + h
                        pe.wait_ge(rt_ready, (g + 1) * KC)
                        for m in range(KC):
                            for j in range(TC):
                                mm = nc.tensor.transpose(TP[m][:, j * P:(j + 1) * P],
                                                         R[k][:, h * TC + j, m * P:(m + 1) * P], ident)
                            mm.then_inc(t_ready, 1)
                        pe.wait_ge(rt_ready, (g + 2) * KC)
                        for m in range(MH):
                            pe.wait_ge(r_done, g * MH + m + 1)
                            for q in range(KC):
                                mm = nc.tensor.matmul(HP[m % 2][:, :], W1[k][:, q, m * P:(m + 1) * P], RT[:, q, :],
                                                      start=(q == 0), stop=(q == KC - 1))
                            mm.then_inc(h_ready, 1)
                        pe.wait_ge(r_done, (g + 1) * MH + 2)
                        for j in range(TC):
                            if j % 2 == 0:
                                pe.wait_ge(o_copied, g * 2 + j // 2 + 9)
                            for m in range(MH):
                                mm = nc.tensor.matmul(OP[j // 2][:, j % 2 * C:(j % 2 + 1) * C],
                                                      H[:, m, j * P:(j + 1) * P], W2[k][:, m, :], start=(m == 0),
                                                      stop=(m == MH - 1))
                            if j % 2:
                                mm.then_inc(o_ready, 1)

        @block.scalar
        def _(act):
            act.sem_inc(rt_ready, KC)
            act.sem_inc(r_done, 2)
            for h in range(2):
                act.sem_inc(stored[h], 16)
            with act.Fori(0, E1 // 2) as i:
                for k in range(2):
                    act.wait_ge(loaded[k], (i + 1) * 80)
                    for h in range(2):
                        g = 4 * i + 2 * k + h
                        for m in range(KC):
                            act.wait_ge(t_ready, g * KC + m + 1)
                            nc.scalar.copy(RT[:, m, :], TP[m][:, :]).then_inc(rt_ready, 1)
                        for m in range(MH):
                            act.wait_ge(h_ready, g * MH + m + 1)
                            act.wait_ge(o_copied, g * 2 + 10)
                            nc.scalar.activation(H[:, m, :], HP[m % 2][:, :], ACT.Relu, bias=B1[k][:, m:m + 1])\
                                .then_inc(r_done, 1)

        @block.vector
        def _(dve):
            dve.sem_inc(o_copied, 10)
            with dve.Fori(0, E1 // 2) as i:
                for k in range(2):
                    dve.wait_ge(loaded[k], (i + 1) * 80)
                    for h in range(2):
                        g = 4 * i + 2 * k + h
                        for a in range(2):
                            dve.wait_ge(stored[h], (2 * i + k + 1) * 16)
                            dve.wait_ge(o_ready, g * 2 + a + 1)
                            nc.vector.tensor_tensor(O[h][:, 2 * a:2 * a + 2, :],
                                                    OP[a][:, :].rearrange("p (a c) -> p a c", a=2),
                                                    B2[k][:, :].unsqueeze(1).to_broadcast([P, 2, C]), ALU.add)\
                                .then_inc(o_copied, 1)


def combine_phase(nc, SLOTS, WEIGHTS, EOUT, X, out):
    NR = 4
    with Phase(nc, "combine") as ph:
        G = [ph.sb(f"rows{k}", [P, 2, C]) for k in range(NR)]
        gathered = [ph.sem(f"rows_in{k}") for k in range(NR)]
        added, first, stored = ph.sem("rows_added"), ph.sem("first_added"), ph.sem("out_stored")
        block = ph.block()

        @block.gpsimd
        def _(pool):
            for t in range(NT):
                if t >= NR:
                    pool.wait_ge(added, t - NR + 1)
                for k in range(2):
                    pool.indirect_dma_start(G[t % NR][:, k, :], None, EOUT,
                                            bass.IndirectOffsetOnAxis(ap=SLOTS[:, 2 + k, t:t + 1], axis=0),
                                            bounds_check=E1 * CAP - 1, oob_is_err=False).then_inc(gathered[t % NR], 16)

        @block.vector
        def _(dve):
            for t in range(NT):
                dve.wait_ge(gathered[t % NR], 32 * (t // NR + 1))
                for k in range(2):
                    ins = nc.vector.scalar_tensor_tensor(X[:, t, :], G[t % NR][:, k, :], WEIGHTS[:, k, t:t + 1],
                                                         X[:, t, :], ALU.mult, ALU.add)
                    if k == 0:
                        ins.then_inc(first, 1)
                        dve.wait_ge(first, t + 1)
                ins.then_inc(added, 1)

        @block.sync
        def _(sp):
            rows = out.rearrange("a (n p) c -> p (a n) c", p=P)
            for n in range(NCH):
                sp.wait_ge(added, (n + 1) * TC)
                sp.dma_start(rows[:, n * TC:(n + 1) * TC, :], X[:, n * TC:(n + 1) * TC, :]).then_inc(stored, 16)
            sp.wait_ge(stored, NCH * 16)


def build(nc, ins, out):
    with ExitStack() as whole:
        def sb(name, shape, dt=F32, stack=whole, side="left"):
            return stack.enter_context(nc.sbuf_tensor(name, shape, dt, side=side))

        q_scratch = nc.dram_tensor("q_scratch", (2, C, T), F32).ap()
        k_scratch = nc.dram_tensor("k_scratch", (2, C, T), F32).ap()
        DISP = nc.dram_tensor("expert_rows", (E1 * CAP, C), F32).ap()
        EOUT = nc.dram_tensor("expert_out", (E1 * CAP, C), F32).ap()
        L0, L1 = (lambda name: ins["L0_" + name]), (lambda name: ins["L1_" + name])

        CST = sb("constants", [P, CONSTS])
        X = sb("residual", [P, NT, C])
        V = sb("values", [P, NT, C])
        with ExitStack() as stack:
            XN = sb("xn", [P, NT, C], stack=stack)
            XNT = sb("xn_t", [P, KC, T], stack=stack)
            SC = sb("gate_scores", [P, E0, NT], stack=stack)
            front_phase(nc, L0("attn_x")[0], L0("attn_W_down"),
                        (L0("attn_toqueries"), L0("attn_tokeys"), L0("attn_tovalues")), L0("ffn_wg"), L0("ffn_bg"),
                        ins["constants"], CST, X, XN, XNT, V, SC, q_scratch, k_scratch)
            MASKT = sb("expert_mask_t", [E0, T], BF16, stack=stack)
            select_phase(nc, CST, SC, MASKT)
            ffn0_phase(nc, L0("ffn_w1"), L0("ffn_b1"), L0("ffn_w2"), L0("ffn_b2"), L0("ffn_gamma"), L0("ffn_beta"),
                       L0("attn_b_unify"), CST, MASKT, X, XN, XNT)
        LG = sb("router_logits", [P, E1, NT])
        SLOTS = sb("slots", [P, 4, NT], I32)
        WEIGHTS = sb("expert_weights", [P, 2, NT])
        XN1 = V
        with ExitStack() as left:
            with ExitStack() as right, ExitStack() as top:
                with ExitStack() as attention:
                    ATT = sb("attention", [P, 1 + HEADS * NCH, TC * D], stack=attention, side="right")
                    attention_phase(nc, q_scratch, k_scratch, V, ATT, CST)
                    XT1 = sb("xn1_t", [P, KC, T], stack=left)
                    YT = sb("y_t", [P, KC, T + 2], stack=top)
                    unify_phase(nc, L0("attn_W_unify"), L1("attn_norm_w"), CST, ATT, X, XN1, XT1, YT, DISP)
                X2T = sb("x2_t", [P, KC, T], stack=right, side="right")
                router_phase(nc, L1("ffn_rw1"), L1("ffn_rb1"), L1("ffn_rw2"), L1("ffn_rb2"), L1("attn_conv_w"),
                             L1("attn_conv_b"), L1("attn_a"), L1("attn_b"), CST, XT1, YT, X2T, LG)
                top.close()
                dispatch_phase(nc, CST, LG, SLOTS, WEIGHTS)
                ZT = XT1
                z_phase(nc, L1("attn_mlp_norm_w"), CST, X2T, ZT)
                mlp_phase(nc, L1("attn_w_gate"), L1("attn_b_gate"), L1("attn_w_up"), L1("attn_b_up"),
                          L1("attn_w_down"), L1("attn_b_down"), CST, ZT, X2T, X, XN1, SLOTS, DISP)
        expert_phase(nc, L1("ffn_ew1"), L1("ffn_eb1"), L1("ffn_ew2"), L1("ffn_eb2"), CST, DISP, EOUT)
        combine_phase(nc, SLOTS, WEIGHTS, EOUT, X, out)


def constants():
    import numpy as np

    p = np.arange(P)[:, None]
    c = np.zeros((P, CONSTS), np.float32)
    c[:, IDENT:IDENT + P] = p == np.arange(P)
    c[:, SUMCOL:SUMCOL + D + 1] = p % 32 == np.arange(D + 1)
    c[:, DIAG8:DIAG8 + 8] = p // D == np.arange(8)
    c[:, BEFORE:BEFORE + P] = p < np.arange(P)
    c[:, ONES:ONES + P] = 1
    c[:, RESET:RESET + E0 * NT] = np.arange(E0 * NT) % NT != 0
    c[:, IOTA:IOTA + E0 * NT] = np.arange(E0 * NT) // NT
    m, q = np.arange(F0) // P, np.arange(F0) % P
    c[:, EXPAND:EXPAND + F0] = p == 2 * m + q // (F0 // E0)
    return c


def kernel(**inputs):
    import numpy as np
    import concourse.bacc as bacc
    from concourse.bass_utils import run_bass_kernel_spmd

    nc = bacc.Bacc("TRN2", target_bir_lowering=False, num_devices=1)
    arrays = {name: np.ascontiguousarray(a) for name, a in inputs.items()}
    arrays["constants"] = constants()
    arrays = {f"in_{name}": a for name, a in arrays.items()}
    ins = {name[3:]: nc.dram_tensor(name, a.shape, mybir.dt.from_np(a.dtype), kind="ExternalInput").ap()
           for name, a in arrays.items()}
    out = nc.dram_tensor("out_0", (1, T, C), F32, kind="ExternalOutput").ap()
    build(nc, ins, out)
    result = run_bass_kernel_spmd(nc, [arrays], core_ids=[0])
    return result.results[0]["out_0"]
```

```python
from contextlib import ExitStack

import concourse.bass as bass
from concourse import mybir

F32 = mybir.dt.float32
F32R = mybir.dt.float32r
BF16 = mybir.dt.bfloat16
I32 = mybir.dt.int32
U32 = mybir.dt.uint32
ALU = mybir.AluOpType
ACT = mybir.ActivationFunctionType
AX = mybir.AxisListType

P = 128
T = 4096
C = 256
KC = C // P
NT = T // P
CH = 512
NCH = T // CH
TC = CH // P
HEADS = 16
D = C // HEADS
LN_EPS = 1e-5
E0 = 16
KEEP0 = T // 2
F0 = 1024
E1 = 8
CAP = 1024
HID = 1024
MH = HID // P

IDENT, SUMCOL, DIAG8, BEFORE, ONES, RESET, IOTA, EXPAND, CONSTS = 0, 128, 145, 153, 281, 409, 921, 1433, 2457


class Chain:

    def __init__(self, engine, semaphore):
        self.engine, self.semaphore, self.base, self.n = engine, semaphore, 0, 0

    def start(self, base):
        self.base, self.n = base, 0

    def __call__(self, instruction):
        self.n += 1
        instruction.then_inc(self.semaphore, 1)
        self.engine.wait_ge(self.semaphore, self.base + self.n)


class Phase:

    def __init__(self, nc, name):
        self.nc, self.name, self.stack = nc, name, ExitStack()

    def __enter__(self):
        return self

    def __exit__(self, *what):
        return self.stack.__exit__(*what)

    def sb(self, name, shape, dt=F32):
        return self.stack.enter_context(self.nc.sbuf_tensor(f"{self.name}_{name}", shape, dt))

    def ps(self, name, shape=(P, CH), dt=F32):
        return self.stack.enter_context(self.nc.psum_tensor(f"{self.name}_{name}_sums", list(shape), dt))

    def sem(self, name):
        return self.stack.enter_context(self.nc.semaphore(f"{self.name}_{name}"))

    def block(self):
        return self.stack.enter_context(self.nc.Block())


def front_phase(nc, x, w_down, head_weights, wg, bg, consts, CST, X, XN, XNT, V, SC, q_scratch, k_scratch):
    with Phase(nc, "front") as ph:
        WD = ph.sb("w_down", [P, KC, C])
        WG = ph.sb("w_gate", [P, KC, E0])
        BG = ph.sb("b_gate", [P, E0])
        HW = ph.sb("head_weights", [P, 3, KC, D])
        BLK = ph.sb("block_diagonal", [P, 3 * KC, P])
        BD = ph.sb("block_diagonal_t", [P, 3 * KC, P])
        STATS = ph.sb("stats", [P, TC, 6])
        MV = ph.sb("mean_var", [P, TC, 2])
        VAR = ph.sb("variance", [P, TC])
        STD = ph.sb("deviation", [P, TC])
        RSTD = ph.sb("rstd", [P, TC])
        XG = [ph.sb(f"xn_chunk{k}", [P, TC, C]) for k in range(2)]
        XT = [ph.sb(f"xn_t_chunk{k}", [P, KC, CH]) for k in range(2)]
        XD = ph.sb("x_down_t", [P, KC, CH])
        HI = [ph.sb(f"high{k}", [P, 4, CH], F32R) for k in range(2)]
        LO = [ph.sb(f"low{k}", [P, 4, CH], F32R) for k in range(2)]
        TP = [ph.ps(f"transposed{k}") for k in range(KC)]
        XDP = [ph.ps(f"x_down{k}") for k in range(KC)]
        QKP = [ph.ps(f"queries_keys{k}") for k in range(2)]
        VP = ph.ps("values")
        GP = ph.ps("gate")

        cst_in = ph.sem("constants_in")
        w_in = ph.sem("weights_in")
        x_in = [ph.sem(f"x_in{k}") for k in range(2)]
        ln_done = ph.sem("x_normalised")
        stats_ready = ph.sem("stats_ready")
        var_ready = ph.sem("variance_ready")
        std_ready = ph.sem("deviation_ready")
        xg_ready = ph.sem("xn_ready")
        t_ready = ph.sem("transposed_ready")
        xt_ready = ph.sem("xn_t_ready")
        stored = [ph.sem(f"xn_stored{k}") for k in range(2)]
        xd_ready = ph.sem("x_down_ready")
        xd_copied = ph.sem("x_down_copied")
        qk_ready = ph.sem("queries_keys_ready")
        hi_done = ph.sem("high_done")
        lo_done = ph.sem("low_done")
        parts_out = [ph.sem(f"parts_out{k}") for k in range(2)]
        v_ready = ph.sem("values_ready")
        v_copied = ph.sem("values_copied")
        g_ready = ph.sem("gate_ready")
        g_copied = ph.sem("gate_copied")
        blk_ready = ph.sem("blocks_ready")
        bd_ready = ph.sem("block_transposes_ready")
        bd_copied = ph.sem("block_transposes_copied")
        dchain = ph.sem("vector_chain")
        block = ph.block()

        @block.sync
        def _(sp):
            sp.dma_start(CST[:, :], consts[:, 0:EXPAND]).then_inc(cst_in, 16)
            for n, w in enumerate(head_weights):
                sp.dma_start(HW[:, n, :, :], w.rearrange("(m h) i k -> (h i) m k", m=KC)).then_inc(w_in, 16)
            sp.dma_start(WD[:, :, :], w_down.rearrange("(k p) n -> p k n", p=P)).then_inc(w_in, 16)
            sp.dma_start(WG[:, :, :], wg.rearrange("(k p) n -> p k n", p=P)).then_inc(w_in, 16)
            sp.dma_start(BG[:, :], bg.rearrange("(a n) -> a n", a=1).to_broadcast([P, E0])).then_inc(w_in, 16)
            with sp.Fori(0, NCH // 2) as i:
                for k in range(2):
                    n = 2 * i + k
                    sp.wait_ge(xg_ready, (n + 1) * TC)
                    sp.dma_start(XN[:, bass.ds(n * TC, TC), :], XG[k][:, :, :]).then_inc(stored[k], 16)
                    sp.wait_ge(xt_ready, (n + 2) * KC)
                    sp.dma_start(XNT[:, :, bass.ds(n * CH, CH)], XT[k][:, :, :]).then_inc(stored[k], 16)
                    sp.wait_ge(lo_done, (n + 1) * 4 + 2)
                    for m in range(KC):
                        for part, src in enumerate((HI[k], LO[k])):
                            for out, scratch in enumerate((q_scratch, k_scratch)):
                                sp.dma_start(scratch[part, m * P:(m + 1) * P, bass.ds(n * CH, CH)],
                                               src[:, 2 * out + m, :].bitcast(F32)).then_inc(parts_out[k], 16)
            for k in range(2):
                sp.wait_ge(stored[k], 32 * (NCH // 2) + 16)
                sp.wait_ge(parts_out[k], 128 * (NCH // 2) + 16)

        @block.gpsimd
        def _(pool):
            xr = x.rearrange("(n p) c -> p n c", p=P)
            with pool.Fori(0, NCH // 2) as i:
                for k in range(2):
                    n = 2 * i + k
                    pool.wait_ge(ln_done, n + 1)
                    pool.dma_start(X[:, bass.ds(n * TC, TC), :], xr[:, bass.ds(n * TC, TC), :]).then_inc(x_in[k], 16)

        @block.tensor
        def _(pe):
            ident = CST[:, IDENT:IDENT + P]
            pe.wait_ge(blk_ready, 3 * KC)
            for n in range(3 * KC):
                if n >= 2:
                    pe.wait_ge(bd_copied, n - 1)
                nc.tensor.transpose(QKP[n % 2][:, 0:P], BLK[:, n, :], ident).then_inc(bd_ready, 1)
            pe.wait_ge(bd_copied, 3 * KC)
            pe.wait_ge(w_in, 96)
            with pe.Fori(0, NCH // 2) as i:
                for k in range(2):
                    n = 2 * i + k
                    pe.wait_ge(xg_ready, (n + 1) * TC)
                    pe.wait_ge(xt_ready, (n + 1) * KC)
                    for m in range(KC):
                        for j in range(TC):
                            mm = nc.tensor.transpose(TP[m][:, j * P:(j + 1) * P], XG[k][:, j, m * P:(m + 1) * P],
                                                     ident)
                        mm.then_inc(t_ready, 1)
                    pe.wait_ge(xt_ready, (n + 2) * KC)
                    for m in range(KC):
                        pe.wait_ge(xd_copied, n * KC + m + 1)
                        for q in range(KC):
                            mm = nc.tensor.matmul(XDP[m][:, :], WD[:, q, m * P:(m + 1) * P], XT[k][:, q, :],
                                                  start=(q == 0), stop=(q == KC - 1))
                        mm.then_inc(xd_ready, 1)
                    pe.wait_ge(g_copied, n + 1)
                    for j in range(TC):
                        for q in range(KC):
                            mm = nc.tensor.matmul(GP[:, j * E0:(j + 1) * E0], XT[k][:, q, j * P:(j + 1) * P],
                                                  WG[:, q, :], start=(q == 0), stop=(q == KC - 1))
                    mm.then_inc(g_ready, 1)
                    pe.wait_ge(xd_copied, (n + 2) * KC)
                    for o in range(2 * KC):
                        pe.wait_ge(lo_done, n * 4 + o + 1)
                        nc.tensor.matmul(QKP[o % 2][:, :], BD[:, o, :], XD[:, o % KC, :], start=True, stop=True)\
                            .then_inc(qk_ready, 1)
                    for half in range(2):
                        pe.wait_ge(v_copied, n * 2 + half + 1)
                        for j in range(2):
                            for m in range(KC):
                                t = (2 * half + j) * P
                                mm = nc.tensor.matmul(VP[:, j * C + m * P:j * C + (m + 1) * P], XD[:, m, t:t + P],
                                                      BD[:, 2 * KC + m, :], start=True, stop=True)
                        mm.then_inc(v_ready, 1)

        @block.scalar
        def _(act):
            act.sem_inc(xt_ready, KC)
            act.sem_inc(xd_copied, KC)
            act.sem_inc(v_copied, 1)
            for k in range(2):
                act.sem_inc(stored[k], 16)
                act.sem_inc(parts_out[k], 16)
            for n in range(3 * KC):
                act.wait_ge(bd_ready, n + 1)
                nc.scalar.copy(BD[:, n, :], QKP[n % 2][:, 0:P]).then_inc(bd_copied, 1)
            with act.Fori(0, NCH // 2) as i:
                for k in range(2):
                    n = 2 * i + k
                    act.wait_ge(var_ready, n + 1)
                    nc.scalar.activation(STD[:, :], VAR[:, :], ACT.Sqrt).then_inc(std_ready, 1)
                    act.wait_ge(stored[k], 32 * i + 16)
                    for m in range(KC):
                        act.wait_ge(t_ready, n * KC + m + 1)
                        nc.scalar.copy(XT[k][:, m, :], TP[m][:, :]).then_inc(xt_ready, 1)
                    for m in range(KC):
                        act.wait_ge(xd_ready, n * KC + m + 1)
                        nc.scalar.copy(XD[:, m, :], XDP[m][:, :]).then_inc(xd_copied, 1)
                    act.wait_ge(parts_out[k], 128 * i + 16)
                    for o in range(2 * KC):
                        act.wait_ge(qk_ready, n * 4 + o + 1)
                        nc.scalar.mul(HI[k][:, o, :], QKP[o % 2][:, :], D ** -0.25).then_inc(hi_done, 1)
                    for half in range(2):
                        act.wait_ge(v_ready, n * 2 + half + 1)
                        nc.scalar.copy(V[:, bass.ds(n * TC + half * 2, 2), :].rearrange("p j c -> p (j c)"), VP[:, :])\
                            .then_inc(v_copied, 1)

        @block.vector
        def _(dve):
            link = Chain(dve, dchain)
            dve.sem_inc(ln_done, 2)
            dve.sem_inc(lo_done, 2)
            dve.sem_inc(g_copied, 1)
            dve.wait_ge(cst_in, 16)
            dve.wait_ge(w_in, 96)
            diag = CST[:, DIAG8:DIAG8 + 8].unsqueeze(2).to_broadcast([P, 8, D])
            for n in range(3 * KC):
                dense = HW[:, n // KC, n % KC, :].unsqueeze(1).to_broadcast([P, 8, D])
                nc.vector.tensor_tensor(BLK[:, n, :].rearrange("p (h k) -> p h k", k=D), dense, diag, ALU.mult)\
                    .then_inc(blk_ready, 1)
            with dve.Fori(0, NCH // 2) as i:
                link.start(i * 8)
                for k in range(2):
                    n = 2 * i + k
                    dve.wait_ge(x_in[k], (i + 1) * 16)
                    for j in range(TC):
                        ins = nc.vector.bn_stats(STATS[:, j, :], X[:, bass.ds(n * TC + j, 1), :].rearrange("p a c -> p (a c)"))
                    link(ins)
                    dve.sem_inc(stats_ready, 1)
                    for j in range(TC):
                        ins = nc.vector.bn_aggr(MV[:, j, :], STATS[:, j, :])
                    link(ins)
                    link(nc.vector.tensor_scalar(VAR[:, :], MV[:, :, 1], LN_EPS, None, ALU.add))
                    dve.sem_inc(var_ready, 1)
                    dve.wait_ge(std_ready, n + 1)
                    link(nc.vector.reciprocal(RSTD[:, :], STD[:, :]))
                    dve.wait_ge(stored[k], 32 * i + 16)
                    for j in range(TC):
                        nc.vector.tensor_scalar(XG[k][:, j, :], X[:, bass.ds(n * TC + j, 1), :].rearrange("p a c -> p (a c)"),
                                                MV[:, j, 0:1], RSTD[:, j:j + 1], ALU.subtract, ALU.mult)\
                            .then_inc(xg_ready, 1)
                    dve.sem_inc(ln_done, 1)
                    dve.wait_ge(g_ready, n + 1)
                    nc.vector.tensor_tensor(SC[:, :, bass.ds(n * TC, TC)].rearrange("p e t -> p t e"),
                                            GP[:, 0:TC * E0].rearrange("p (t e) -> p t e", e=E0),
                                            BG[:, :].unsqueeze(1).to_broadcast([P, TC, E0]), ALU.add)\
                        .then_inc(g_copied, 1)
                    for o in range(2 * KC):
                        dve.wait_ge(hi_done, n * 4 + o + 1)
                        nc.vector.scalar_tensor_tensor(LO[k][:, o, :], QKP[o % 2][:, :], D ** -0.25,
                                                       HI[k][:, o, :].bitcast(F32), ALU.mult, ALU.subtract)\
                            .then_inc(lo_done, 1)



def top_two(nc, link, CST, S, ne, low, work):
    FIRST, SECOND, EQ, REST, BEST1, BEST2, INDEX = work
    iota = CST[:, IOTA:IOTA + ne * NT].rearrange("p (e t) -> p e t", t=NT)

    def per_token(a):
        return a[:, :].unsqueeze(1).to_broadcast([P, ne, NT])

    def over_experts(a):
        return a[:, :, :].rearrange("p e t -> p t e")

    for scores, best, hot in ((S, BEST1, FIRST), (REST, BEST2, SECOND)):
        link(nc.vector.tensor_reduce(best[:, :], over_experts(scores), AX.X, ALU.max))
        link(nc.vector.tensor_tensor(EQ[:, :, :], scores[:, :, :], per_token(best), ALU.is_equal))
        link(nc.vector.scalar_tensor_tensor(EQ[:, :, :], iota, -64.0, EQ[:, :, :], ALU.add, ALU.mult))
        link(nc.vector.tensor_reduce(INDEX[:, :], over_experts(EQ), AX.X, ALU.min))
        link(nc.vector.scalar_tensor_tensor(hot[:, :, :], iota, -64.0, per_token(INDEX), ALU.add, ALU.is_equal))
        if hot is FIRST:
            link(nc.vector.scalar_tensor_tensor(REST[:, :, :], hot[:, :, :], low, S[:, :, :], ALU.mult, ALU.add))

class Ranks:

    def __init__(self, ph, ne):
        self.ne = ne
        self.BEFORE_P, self.TOTAL_P = ph.ps("before_in_tile"), ph.ps("tile_totals")
        self.TOTAL = ph.sb("tile_totals_sb", [P, ne * NT])
        self.SUM = ph.sb("tile_sums", [P, ne * NT])
        self.mask_ready, self.counted = ph.sem("rank_mask_ready"), ph.sem("rank_counted")

    def count(self, nc, pe, CST, MASK):
        w = self.ne * NT
        pe.wait_ge(self.mask_ready, 1)
        mask = MASK[:, :, :].rearrange("p e t -> p (e t)")
        nc.tensor.matmul(self.BEFORE_P[:, 0:w], CST[:, BEFORE:BEFORE + P], mask, start=True, stop=True)
        nc.tensor.matmul(self.TOTAL_P[:, 0:w], CST[:, ONES:ONES + P], mask, start=True, stop=True)\
            .then_inc(self.counted, 1)

    def finish(self, nc, dve, link, CST, RANK):
        w = self.ne * NT
        dve.wait_ge(self.counted, 1)
        rank = RANK[:, :, :].rearrange("p e t -> p (e t)")
        link(nc.vector.tensor_copy(self.TOTAL[:, :], self.TOTAL_P[:, 0:w]))
        link(nc.vector.tensor_tensor_scan(self.SUM[:, :], CST[:, RESET:RESET + w], self.TOTAL[:, :], 0.0, ALU.mult,
                                          ALU.add))
        link(nc.vector.tensor_tensor(self.SUM[:, :], self.SUM[:, :], self.TOTAL[:, :], ALU.subtract))
        link(nc.vector.tensor_tensor(rank, self.SUM[:, :], self.BEFORE_P[:, 0:w], ALU.add))

def select_phase(nc, CST, SC, MASKT):
    BITS = 30
    with Phase(nc, "select") as ph:
        shape = [P, E0, NT]
        FIRST, SECOND, EQ, REST, ROUTE, GE = (ph.sb(n, shape) for n in ("first", "second", "eq", "rest", "route", "ge"))
        BEST1, BEST2, INDEX, TOK = (ph.sb(n, [P, NT]) for n in ("best1", "best2", "index", "token"))
        CUR, CAND, BIT, TAKE = (ph.sb(n, [P, E0], I32) for n in ("threshold", "candidate", "bit", "take"))
        COUNT, NEED = ph.sb("count", [P, E0]), ph.sb("need", [P, E0])
        MASK = ph.sb("mask", shape, BF16)
        LARGE = ph.sb("large", shape, I32)
        IDB = ph.sb("ident_bf16", [P, P], BF16)
        TOTALS = ph.ps("totals")
        MT = [ph.ps(f"mask_t{k}", dt=BF16) for k in range(2)]
        ranks = Ranks(ph, E0)
        shifted, exps, counted, summed = (ph.sem(n) for n in ("shifted", "exps", "counts_ready", "counts_summed"))
        mask_ready, mt_ready, mt_copied, dchain = (ph.sem(n) for n in
                                                   ("mask_ready", "mask_t_ready", "mask_t_copied", "vector_chain"))
        block = ph.block()

        def per_token(a):
            return a[:, :].unsqueeze(1).to_broadcast(shape)

        def per_expert(a):
            return a.unsqueeze(2).to_broadcast(shape)

        @block.scalar
        def _(act):
            act.wait_ge(shifted, 1)
            nc.scalar.activation(ROUTE[:, :, :], ROUTE[:, :, :], ACT.Exp).then_inc(exps, 1)

        @block.tensor
        def _(pe):
            with pe.Fori(0, BITS + 1) as i:
                pe.wait_ge(counted, i + 1)
                nc.tensor.matmul(TOTALS[:, 0:E0], CST[:, ONES:ONES + P], COUNT[:, :], start=True, stop=True)\
                    .then_inc(summed, 1)
            ranks.count(nc, pe, CST, GE)
            pe.wait_ge(mask_ready, 1)
            for t in range(NT):
                if t % 4 == 0 and t >= 8:
                    pe.wait_ge(mt_copied, t // 4 - 1)
                mm = nc.tensor.transpose(MT[t // 4 % 2][0:E0, t % 4 * P:(t % 4 + 1) * P], MASK[:, :, t], IDB[:, :])
                if t % 4 == 3:
                    mm.then_inc(mt_ready, 1)

        @block.vector
        def _(dve):
            link = Chain(dve, dchain)
            link(nc.vector.tensor_copy(IDB[:, :], CST[:, IDENT:IDENT + P]))
            link(nc.vector.tensor_reduce(TOK[:, :], SC[:, :, :].rearrange("p e t -> p t e"), AX.X, ALU.max))
            nc.vector.tensor_tensor(ROUTE[:, :, :], SC[:, :, :], per_token(TOK), ALU.subtract).then_inc(shifted, 1)
            dve.wait_ge(exps, 1)
            link(nc.vector.tensor_reduce(TOK[:, :], ROUTE[:, :, :].rearrange("p e t -> p t e"), AX.X, ALU.add))
            link(nc.vector.reciprocal(TOK[:, :], TOK[:, :]))
            link(nc.vector.tensor_tensor(ROUTE[:, :, :], ROUTE[:, :, :], per_token(TOK), ALU.mult))
            top_two(nc, link, CST, ROUTE, E0, -4.0, (FIRST, SECOND, EQ, REST, BEST1, BEST2, INDEX))
            link(nc.vector.tensor_tensor(FIRST[:, :, :], FIRST[:, :, :], SECOND[:, :, :], ALU.add))
            link(nc.vector.tensor_tensor(ROUTE[:, :, :], ROUTE[:, :, :], FIRST[:, :, :], ALU.mult))
            link(nc.vector.tensor_scalar(REST[:, :, :], ROUTE[:, :, :], 1e-6, None, ALU.add))
            link(nc.vector.reciprocal(SECOND[:, :, :], REST[:, :, :]))
            link(nc.vector.tensor_scalar(LARGE[:, :, :], ROUTE[:, :, :], 2.0 ** -10, None, ALU.is_ge))
            link(nc.vector.tensor_tensor(GE[:, :, :], REST[:, :, :], ROUTE[:, :, :], ALU.subtract))
            link(nc.vector.tensor_tensor(GE[:, :, :], GE[:, :, :], SECOND[:, :, :], ALU.mult))
            link(nc.vector.tensor_scalar(GE[:, :, :], GE[:, :, :], -1.0, 1.0, ALU.mult, ALU.add))
            link(nc.vector.tensor_tensor(ROUTE[:, :, :], ROUTE[:, :, :], SECOND[:, :, :], ALU.mult))
            link(nc.vector.copy_predicated(ROUTE[:, :, :], LARGE[:, :, :], GE[:, :, :]))
            link(nc.vector.memset(CUR[:, :], 0))
            link(nc.vector.memset(BIT[:, :], 1 << (BITS - 1)))
            start, loop = link.n, 8
            with dve.Fori(0, BITS) as i:
                link.start(start + i * loop)
                link(nc.vector.tensor_tensor(CAND[:, :], CUR[:, :], BIT[:, :], ALU.bitwise_or))
                link(nc.vector.tensor_tensor(GE[:, :, :], ROUTE[:, :, :], per_expert(CAND[:, :].bitcast(F32)), ALU.is_ge))
                link(nc.vector.tensor_reduce(COUNT[:, :], GE[:, :, :], AX.X, ALU.add))
                dve.sem_inc(counted, 1)
                dve.wait_ge(summed, i + 1)
                link(nc.vector.tensor_scalar(NEED[:, :], TOTALS[:, 0:E0], KEEP0 - 0.5, -1.0, ALU.is_ge, ALU.mult))
                link(nc.vector.tensor_copy(TAKE[:, :], NEED[:, :]))
                link(nc.vector.tensor_tensor(TAKE[:, :], TAKE[:, :], BIT[:, :], ALU.bitwise_and))
                link(nc.vector.tensor_tensor(CUR[:, :], CUR[:, :], TAKE[:, :], ALU.bitwise_or))
                link(nc.vector.tensor_scalar(BIT[:, :], BIT[:, :], 1, None, ALU.logical_shift_right))
            link.start(start + BITS * loop)
            threshold = per_expert(CUR[:, :].bitcast(F32))
            link(nc.vector.tensor_tensor(FIRST[:, :, :], ROUTE[:, :, :], threshold, ALU.is_gt))
            link(nc.vector.tensor_reduce(COUNT[:, :], FIRST[:, :, :], AX.X, ALU.add))
            dve.sem_inc(counted, 1)
            dve.wait_ge(summed, BITS + 1)
            link(nc.vector.tensor_scalar(NEED[:, :], TOTALS[:, 0:E0], -1.0, float(KEEP0), ALU.mult, ALU.add))
            link(nc.vector.tensor_tensor(GE[:, :, :], ROUTE[:, :, :], threshold, ALU.is_equal))
            dve.sem_inc(ranks.mask_ready, 1)
            ranks.finish(nc, dve, link, CST, REST)
            link(nc.vector.tensor_tensor(REST[:, :, :], REST[:, :, :], per_expert(NEED[:, :]), ALU.is_lt))
            link(nc.vector.tensor_tensor(REST[:, :, :], REST[:, :, :], GE[:, :, :], ALU.mult))
            nc.vector.tensor_tensor(MASK[:, :, :], FIRST[:, :, :], REST[:, :, :], ALU.add).then_inc(mask_ready, 1)
            for n in range(NT // 4):
                dve.wait_ge(mt_ready, n + 1)
                nc.vector.tensor_copy(MASKT[:, n * CH:(n + 1) * CH], MT[n % 2][0:E0, :]).then_inc(mt_copied, 1)

def ffn0_phase(nc, w1, b1, w2, b2, gamma, beta, b_unify, consts, MASKT, X, XN, XNT):
    MF = F0 // P
    with Phase(nc, "ffn0") as ph:
        W1 = ph.sb("w1", [P, KC, F0])
        W2 = ph.sb("w2", [P, MF, C])
        B1 = ph.sb("b1", [P, MF])
        B2 = ph.sb("b2", [E0, C])
        ROWS = ph.sb("gamma_beta_bias", [P, 3, C])
        EXP = ph.sb("expand", [E0, MF * P])
        EXPB = ph.sb("expand_bf16", [E0, MF, P], BF16)
        MC = [ph.sb(f"mask_chunk{k}", [E0, CH]) for k in range(2)]
        MCB = [ph.sb(f"mask_chunk_bf16_{k}", [E0, CH], BF16) for k in range(2)]
        G = [ph.sb(f"gelu{k}", [P, CH]) for k in range(2)]
        GM = ph.sb("masked", [P, MF, CH])
        Z = ph.sb("z", [P, TC, C])
        STATS, MV = ph.sb("stats", [P, TC, 6]), ph.sb("mean_var", [P, TC, 2])
        VAR, STD, RSTD = (ph.sb(n, [P, TC]) for n in ("variance", "deviation", "rstd"))
        HP = [ph.ps(f"hidden{k}") for k in range(2)]
        MP = [ph.ps(f"mask{k}") for k in range(2)]
        OP = [ph.ps(f"out{k}") for k in range(2)]
        w_in, h_ready, g_done, m_ready, gm_done = (ph.sem(n) for n in
                                                   ("weights_in", "hidden_ready", "gelu_done", "mask_ready", "masked"))
        out_ready, out_used, exp_ready, mc_ready = (ph.sem(n) for n in
                                                    ("out_ready", "out_used", "expand_ready", "mask_chunk_ready"))
        var_ready, std_ready, stats_ready, dchain = (ph.sem(n) for n in
                                                     ("variance_ready", "deviation_ready", "stats_ready",
                                                      "vector_chain"))
        block = ph.block()

        @block.sync
        def _(sp):
            for k in range(KC):
                sp.dma_start(W1[:, k, :].rearrange("p (e f) -> p e f", e=E0),
                             w1[:, k * P:(k + 1) * P, :].rearrange("e p f -> p e f")).then_inc(w_in, 16)
            sp.dma_start(W2[:, :, :], w2.rearrange("(m a) f n -> (a f) m n", m=MF)).then_inc(w_in, 16)
            sp.dma_start(B1[:, :], b1.rearrange("(m a) f -> (a f) m", m=MF),
                         allow_slow_non_contiguous=True).then_inc(w_in, 16)
            sp.dma_start(B2[:, :], b2).then_inc(w_in, 16)
            sp.dma_start(EXP[:, :], consts[0:E0, EXPAND:EXPAND + MF * P]).then_inc(w_in, 16)
            for n, row in enumerate((gamma, beta, b_unify)):
                sp.dma_start(ROWS[:, n, :], row.rearrange("(a n) -> a n", a=1).to_broadcast([P, C])).then_inc(w_in, 16)
            sp.wait_ge(w_in, 9 * 16)

        @block.gpsimd
        def _(pool):
            with pool.Fori(0, NCH // 2) as i:
                for k in range(2):
                    n = 2 * i + k
                    pool.wait_ge(out_used, n + 1)
                    for chunk in (MC[k], MCB[k]):
                        nc.gpsimd.tensor_copy(chunk[:, :], MASKT[:, bass.ds(n * CH, CH)]).then_inc(mc_ready, 1)

        @block.tensor
        def _(pe):
            pe.wait_ge(w_in, 9 * 16)
            pe.wait_ge(exp_ready, 1)
            with pe.Fori(0, NCH // 2) as i:
                for k in range(2):
                    n = 2 * i + k
                    pe.wait_ge(mc_ready, 2 * (n + 1))
                    for m in range(MF):
                        pe.wait_ge(g_done, n * MF + m + 1)
                        for q in range(KC):
                            mm = nc.tensor.matmul(HP[m % 2][:, :], W1[:, q, m * P:(m + 1) * P],
                                                  XNT[:, q, bass.ds(n * CH, CH)], start=(q == 0), stop=(q == KC - 1))
                        mm.then_inc(h_ready, 1)
                        pe.wait_ge(gm_done, n * MF + m + 1)
                        nc.tensor.matmul(MP[m % 2][:, :], EXPB[:, m, :], MCB[k][:, :],
                                         start=True, stop=True).then_inc(m_ready, 1)
                    pe.wait_ge(gm_done, (n + 1) * MF + 2)
                    pe.wait_ge(out_used, n + 2)
                    for j in range(TC):
                        o = OP[j // 2][:, j % 2 * C:(j % 2 + 1) * C]
                        for m in range(MF):
                            nc.tensor.matmul(o, GM[:, m, j * P:(j + 1) * P], W2[:, m, :], start=(m == 0), stop=False)
                        mm = nc.tensor.matmul(o, MC[k][:, j * P:(j + 1) * P], B2[:, :], start=False, stop=True)
                        mm.then_inc(out_ready, 1)

        @block.scalar
        def _(act):
            act.sem_inc(g_done, 2)
            act.wait_ge(w_in, 9 * 16)
            with act.Fori(0, NCH // 2) as i:
                for k in range(2):
                    n = 2 * i + k
                    for m in range(MF):
                        act.wait_ge(h_ready, n * MF + m + 1)
                        act.wait_ge(gm_done, n * MF + m + 1)
                        nc.scalar.activation(G[m % 2][:, :], HP[m % 2][:, :], ACT.Gelu, bias=B1[:, m:m + 1])\
                            .then_inc(g_done, 1)
                    act.wait_ge(var_ready, n + 1)
                    nc.scalar.activation(STD[:, :], VAR[:, :], ACT.Sqrt).then_inc(std_ready, 1)

        @block.vector
        def _(dve):
            link = Chain(dve, dchain)
            dve.sem_inc(gm_done, 2)
            dve.sem_inc(out_used, 2)
            dve.wait_ge(w_in, 9 * 16)
            nc.vector.tensor_copy(EXPB[:, :, :].rearrange("p m q -> p (m q)"), EXP[:, :]).then_inc(exp_ready, 1)
            with dve.Fori(0, NCH // 2) as i:
                link.start(i * 18)
                for k in range(2):
                    n = 2 * i + k
                    for m in range(MF):
                        dve.wait_ge(g_done, n * MF + m + 3)
                        dve.wait_ge(m_ready, n * MF + m + 1)
                        nc.vector.tensor_tensor(GM[:, m, :], G[m % 2][:, :], MP[m % 2][:, :], ALU.mult)\
                            .then_inc(gm_done, 1)
                    for j in range(0, TC, 2):
                        dve.wait_ge(out_ready, n * TC + j + 2)
                        ins = nc.vector.tensor_tensor(Z[:, j:j + 2, :], OP[j // 2][:, :].rearrange("p (a c) -> p a c", a=2),
                                                      XN[:, bass.ds(n * TC + j, 2), :], ALU.add)
                    link(ins)
                    dve.sem_inc(out_used, 1)
                    for j in range(TC):
                        ins = nc.vector.bn_stats(STATS[:, j, :], Z[:, j, :])
                    link(ins)
                    dve.sem_inc(stats_ready, 1)
                    for j in range(TC):
                        ins = nc.vector.bn_aggr(MV[:, j, :], STATS[:, j, :])
                    link(ins)
                    link(nc.vector.tensor_scalar(VAR[:, :], MV[:, :, 1], LN_EPS, None, ALU.add))
                    dve.sem_inc(var_ready, 1)
                    dve.wait_ge(std_ready, n + 1)
                    link(nc.vector.reciprocal(RSTD[:, :], STD[:, :]))
                    for j in range(TC):
                        ins = nc.vector.tensor_scalar(Z[:, j, :], Z[:, j, :], MV[:, j, 0:1], RSTD[:, j:j + 1],
                                                      ALU.subtract, ALU.mult)
                    link(ins)
                    rows = [ROWS[:, r, :].unsqueeze(1).to_broadcast([P, TC, C]) for r in range(3)]
                    link(nc.vector.tensor_tensor(Z[:, :, :], Z[:, :, :], rows[0], ALU.mult))
                    link(nc.vector.tensor_tensor(Z[:, :, :], Z[:, :, :], rows[1], ALU.add))
                    link(nc.vector.tensor_tensor(Z[:, :, :], Z[:, :, :], rows[2], ALU.add))
                    xs = X[:, bass.ds(n * TC, TC), :]
                    nc.vector.tensor_tensor(xs, xs, Z[:, :, :], ALU.add)


def attention_phase(nc, q_scratch, k_scratch, V, ATT, CST, H=HEADS):
    NCH, NU, NA, NB = T // CH, T // CH, (CH // P) * (T // CH), 3
    R = 2 * NCH
    with Phase(nc, "attention") as ph:
        sb, ps, sem = ph.sb, ph.ps, ph.sem
        QOP = [sb(f"q_operand{b}", [P, T], F32R) for b in range(2)]
        KOP = [sb(f"k_operand{b}", [P, T], F32R) for b in range(2)]
        PR = sb("probs", [P, 8, CH])
        VH = [sb(f"v_head{b}", [P, NT, 32]) for b in range(2)]
        O4 = [sb(f"o_parts{b}", [P, CH]) for b in range(2)]
        MPART = [sb(f"max_parts{b}", [P, 4, 8]) for b in range(2)]
        M4 = sb("row_max", [P, 4])
        MSPLIT = sb("neg_max_split", [P, 4, 2], F32R)
        MROW = [sb(f"neg_max_row{b}", [2, CH], F32R) for b in range(2)]
        RDEN = sb("recip_den", [P, 4])

        ST = [ps(f"scores_t{b}", [P, CH]) for b in range(NB)]
        SA = [ps(f"scores_q{b}", [P, CH]) for b in range(NB)]
        OP = ps("o_psum", [P, CH])
        MISC = ps("misc_psum", [P, CH])

        loaded = [sem(f"operands_loaded{b}") for b in range(2)]
        ones_set = [sem(f"ones_set{b}") for b in range(2)]
        v_set = sem("v_columns_set")
        vh_ready = [sem(f"v_head_ready{b}") for b in range(2)]
        st_ready = sem("scores_ready")
        exp_done = sem("exp_done")
        sa_ready = sem("max_scores_ready")
        red_done = sem("max_part_done")
        pv_done = sem("pv_unit_done")
        o_copied = sem("o_copied")
        msplit = sem("neg_max_split_done")
        mt_ready = sem("neg_max_transposed")
        mrow_copied = sem("neg_max_row_copied")
        mrow_loaded = [sem(f"neg_max_row_loaded{b}") for b in range(2)]
        sel_ready = sem("o_summed")
        norm_done = sem("o_normalised")
        dchain = sem("vector_chain")
        o_init = sem("o_init")
        block = ph.block()
        NI, LOAD = H // 2, 7 * 16
        APART = 2 * R * NA

        def load_head(sp, h, b):
            q, k = QOP[b][:, :].bitcast(F32), KOP[b][:, :].bitcast(F32)
            for row, part_q, part_k in ((0, 1, 0), (D, 0, 0), (2 * D, 0, 1)):
                sp.dma_start(q[row:row + D, :], q_scratch[part_q, bass.ds(h * D, D), :]).then_inc(loaded[b], 16)
                sp.dma_start(k[row:row + D, :], k_scratch[part_k, bass.ds(h * D, D), :]).then_inc(loaded[b], 16)
            sp.dma_start(q[48:50, :], k[50:52, :]).then_inc(loaded[b], 16)

        def load_max_rows(sp, b, c, row, count):
            sp.wait_ge(mrow_copied, count)
            sp.dma_start(QOP[b][48:50, c * CH:(c + 1) * CH].bitcast(F32), MROW[row][:, :].bitcast(F32))\
                .then_inc(mrow_loaded[row], 16)

        def fill(engine, ops, b):
            fills = ((KOP[b][:, :], 0.0), (QOP[b][:, :], 0.0), (KOP[b][32:50, :], 1.0))
            for n, (where, value) in enumerate(fills):
                ops.memset(where.bitcast(F32), value).then_inc(ones_set[b], 1)
                engine.wait_ge(ones_set[b], n + 1)

        @block.sync
        def _(sp):
            sp.wait_ge(ones_set[0], 3)
            load_head(sp, 0, 0)
            load_max_rows(sp, 0, 0, 0, 1)
            sp.wait_ge(ones_set[1], 3)
            with sp.Fori(0, NI) as i:
                for r in range(R):
                    if r == 0:
                        sp.wait_ge(pv_done, i * (R * NU) + 2)
                        load_head(sp, 2 * i + 1, 1)
                    if r == NCH:
                        sp.wait_ge(pv_done, i * (R * NU) + NCH * NU + 2)
                        load_head(sp, (2 * i + 2) % H, 0)
                    n = r + 1
                    load_max_rows(sp, n // NCH % 2, n % NCH, n % 2, i * R + n + 1)
            for b in range(2):
                sp.wait_ge(loaded[b], LOAD * (NI + 1 - b))
                sp.wait_ge(mrow_loaded[b], 16 * (NI * NCH + 1 - b))

        @block.gpsimd
        def _(pool):
            fill(pool, nc.gpsimd, 1)
            fills = [(VH[b][:, :, D:32], 0.0) for b in range(2)] + [(VH[b][:, :, D:D + 1], 1.0) for b in range(2)]
            for n, (where, value) in enumerate(fills):
                nc.gpsimd.memset(where, value).then_inc(v_set, 1)
                pool.wait_ge(v_set, n + 1)

            def stage(h, b):
                nc.gpsimd.tensor_copy(VH[b][:, :, 0:D], V[:, :, bass.ds(h * D, D)]).then_inc(vh_ready[b], 1)

            stage(0, 0)
            stage(1, 1)
            if NI > 1:
                with pool.Fori(0, NI - 1) as i:
                    pool.wait_ge(pv_done, i * (R * NU) + NCH * NU + 2)
                    stage(2 * i + 2, 0)
                    pool.wait_ge(pv_done, i * (R * NU) + R * NU + 2)
                    stage(2 * i + 3, 1)

        @block.tensor
        def _(pe):
            def max_scores(r, a, count):
                b, c, buffer = r // NCH, r % NCH, (r * NA + a) % NB
                qt, k = a // 8, a % 8
                pe.wait_ge(red_done, APART + count + (r * NA + a < (R * NA) % NB))
                nc.tensor.matmul(SA[buffer][:, :], QOP[b][:, c * CH + qt * P:c * CH + (qt + 1) * P],
                                 KOP[b][:, k * CH:(k + 1) * CH],
                                 start=True, stop=True).then_inc(sa_ready, 1)

            def score_tile(r, kt, count):
                b, c, buffer = r // NCH, r % NCH, (r * NT + kt) % NB
                pe.wait_ge(exp_done, count + (r * NT + kt < (R * NT) % NB))
                nc.tensor.matmul(ST[buffer][:, :], KOP[b][:, kt * P:(kt + 1) * P],
                                 QOP[b][:, c * CH:(c + 1) * CH], start=True, stop=True).then_inc(st_ready, 1)

            def pv_unit(b, u, exps):
                pe.wait_ge(exp_done, exps)
                for g in range(4):
                    kt = 4 * u + g
                    mm = nc.tensor.matmul(OP[32 * g:32 * g + 32, :], VH[b][:, kt, :], PR[:, kt % 8, :],
                                          start=(u == 0), stop=(u == NU - 1))
                mm.then_inc(pv_done, 1)

            def transpose_max(count, norms, rows_out):
                pe.wait_ge(msplit, count)
                pe.wait_ge(norm_done, norms)
                if rows_out is not None:
                    pe.wait_ge(mrow_copied, rows_out)
                for j in range(4):
                    mm = nc.tensor.transpose(MISC[0:2, j * P:(j + 1) * P], MSPLIT[:, j, :].bitcast(F32),
                                             CST[:, IDENT:IDENT + P])
                mm.then_inc(mt_ready, 1)

            def sum_parts(par, copies, rows_out):
                pe.wait_ge(o_copied, copies)
                pe.wait_ge(mrow_copied, rows_out)
                for j in range(4):
                    mm = nc.tensor.matmul(MISC[:, j * 32:j * 32 + D + 1], O4[par][:, j * P:(j + 1) * P],
                                          CST[:, SUMCOL:SUMCOL + D + 1], start=True, stop=True)
                mm.then_inc(sel_ready, 1)

            pe.wait_ge(loaded[0], LOAD)
            for a in range(NA):
                max_scores(0, a, a + 1)
            for a in range(NA):
                max_scores(1, a, NA + a + 1)
            transpose_max(1, 1, None)
            pe.wait_ge(mrow_loaded[0], 16)
            for kt in range(4):
                score_tile(0, kt, kt + 1)
            with pe.Fori(0, NI) as i:
                for r in range(R):
                    b = r // NCH
                    if r == NCH - 2:
                        pe.wait_ge(loaded[1], (i + 1) * LOAD)
                    if r == R - 2:
                        pe.wait_ge(loaded[0], (i + 2) * LOAD)
                    if r % NCH == 0:
                        pe.wait_ge(vh_ready[b], i + 1)
                    for u in range(NU):
                        for j in range(4):
                            a, n = 4 * u + j, r * NT + 4 * (u + 1) + j
                            max_scores((r + 2) % R, a, i * (R * NA) + (r + 2) * NA + a + 1)
                            if u == NU - 1 and j == 0:
                                pe.wait_ge(mrow_loaded[(r + 1) % 2], i * (16 * NCH) + 16 * ((r + 1) // 2 + 1))
                            if u < NU - 1:
                                score_tile(r, 4 * (u + 1) + j, i * (R * NT) + n + 1)
                            else:
                                score_tile((r + 1) % R, j, i * (R * NT) + n + 1)
                        if u == 0:
                            pe.wait_ge(o_copied, i * R + r + 1)
                        pv_unit(b, u, i * (R * NT) + r * NT + 4 * u + 4 + NB)
                        if u == 1:
                            transpose_max(i * R + r + 2, i * R + r + 1, i * R + r + 1)
                        if u == 5:
                            sum_parts(r % 2, i * R + r + 1, i * R + r + 2)
            sum_parts(0, NI * R + 1, NI * R + 1)

        @block.scalar
        def _(act):
            act.sem_inc(exp_done, NB)

            def copy_parts(par, units):
                act.wait_ge(pv_done, units)
                nc.scalar.copy(O4[par][:, :], OP[:, :]).then_inc(o_copied, 1)

            def copy_max_rows(row, count):
                act.wait_ge(mt_ready, count)
                nc.scalar.copy(MROW[row][:, :], MISC[0:2, :]).then_inc(mrow_copied, 1)

            copy_max_rows(0, 1)
            act.wait_ge(o_init, 1)
            with act.Fori(0, NI) as i:
                for r in range(R):
                    for kt in range(NT):
                        if kt % 4 == 0:
                            act.wait_ge(pv_done, i * (R * NU) + r * NU + kt // 4 + 1)
                        act.wait_ge(st_ready, i * (R * NT) + r * NT + kt + 1)
                        nc.scalar.activation(PR[:, kt % 8, :], ST[(r * NT + kt) % NB][:, :], ACT.Exp).then_inc(exp_done, 1)
                        if kt == 3:
                            copy_parts(r % 2, i * (R * NU) + r * NU + 2)
                        if kt == 12:
                            copy_max_rows((r + 1) % 2, i * R + r + 2)
            act.wait_ge(exp_done, NI * R * NT + NB)
            act.sem_inc(exp_done, 1)
            copy_parts(0, NI * R * NU + 2)

        @block.vector
        def _(dve):
            fill(dve, nc.vector, 0)
            nc.vector.memset(OP[:, :], 1.0).then_inc(o_init, 1)
            dve.sem_inc(red_done, APART + NB)
            dve.sem_inc(pv_done, 2)
            dve.sem_inc(norm_done, 1)

            def reduce_block(par, a, buffer, count):
                dve.wait_ge(sa_ready, count)
                nc.vector.tensor_reduce(MPART[par][:, a // 8, a % 8:a % 8 + 1], SA[buffer][:, :], AX.X, ALU.max)\
                    .then_inc(red_done, 1)

            def split_max(par, parts, chain):
                dve.wait_ge(red_done, APART + parts)
                nc.vector.tensor_reduce(M4[:, :], MPART[par][:, :, :], AX.X, ALU.max).then_inc(dchain, 1)
                dve.wait_ge(dchain, chain + 1)
                nc.vector.tensor_scalar(MSPLIT[:, :, 0], M4[:, :], -1.0, None, ALU.mult).then_inc(dchain, 1)
                dve.wait_ge(dchain, chain + 2)
                nc.vector.scalar_tensor_tensor(MSPLIT[:, :, 1], M4[:, :], -1.0, MSPLIT[:, :, 0].bitcast(F32), ALU.mult,
                                               ALU.subtract).then_inc(msplit, 1)

            def normalise(slot, sums, chain):
                dve.wait_ge(sel_ready, sums)
                sums4 = MISC[:, 0:P].rearrange("p (j d) -> p j d", j=4)
                nc.vector.reciprocal(RDEN[:, :], sums4[:, :, D]).then_inc(dchain, 1)
                dve.wait_ge(dchain, chain + 1)
                nc.vector.tensor_tensor(ATT[:, slot, :].rearrange("p (j d) -> p j d", d=D), sums4[:, :, 0:D],
                                        RDEN[:, :].unsqueeze(2).to_broadcast([P, 4, D]), ALU.mult)\
                    .then_inc(norm_done, 1)

            for a in range(NA):
                reduce_block(0, a, a % NB, a + 1)
            split_max(0, NA + NB, 0)
            for a in range(NA):
                reduce_block(1, a, (NA + a) % NB, NA + a + 1)
            with dve.Fori(0, NI) as i:
                for r in range(R):
                    dve.wait_ge(mt_ready, i * R + r + 1)
                    split_max((r + 1) % 2, i * (R * NA) + (r + 2) * NA + NB, i * (R * 3) + r * 3 + 2)
                    for a in range(NA):
                        reduce_block(r % 2, a, ((r + 2) % R * NA + a) % NB, i * (R * NA) + (r + 2) * NA + a + 1)
                        if a == 24:
                            normalise(i * R + r, i * R + r + 1, i * (R * 3) + r * 3 + 4)
            normalise(NI * R, NI * R + 1, NI * R * 3 + 2)


def split(nc, link, whole, high, low):
    link(nc.vector.tensor_copy(high, whole))
    return nc.vector.tensor_tensor(low, whole, high.bitcast(F32), ALU.subtract)


def products(nc, out, lhs, rhs, first, last):
    for n, (l, r) in enumerate(((0, 1), (1, 0), (0, 0))):
        mm = nc.tensor.matmul(out, lhs[l], rhs[r], start=first and n == 0, stop=last and n == 2)
    return mm


def unify_phase(nc, w_unify, norm_w, CST, ATT, X, XN1, XT1, YT, DISP):
    with Phase(nc, "unify") as ph:
        WU = ph.sb("w_unify", [P, KC, C])
        NW = ph.sb("norm_w", [P, KC])
        AC = ph.sb("attention_chunk", [P, TC, C])
        AT = ph.sb("attention_t", [P, KC, CH])
        XG = ph.sb("xn_chunk", [P, TC, C])
        YG = ph.sb("y_chunk", [P, TC, C])
        STATS, MV = ph.sb("stats", [P, TC, 6]), ph.sb("mean_var", [P, TC, 2])
        VAR, STD, RSTD, MS, RMS, RRMS = (ph.sb(n, [P, TC]) for n in
                                         ("variance", "deviation", "rstd", "mean_square", "rms", "recip_rms"))
        SQ = ph.sb("squares", [P, C])
        EPS = ph.sb("eps", [P, 1])
        ZERO = ph.sb("zero", [P, 1024])
        TP = [ph.ps(f"transposed{k}") for k in range(KC)]
        UP = [ph.ps(f"unified{k}") for k in range(2)]
        NP = [ph.ps(f"norm_transposed{k}") for k in range(2 * KC)]
        w_in, cleared, zero_set = ph.sem("weights_in"), ph.sem("rows_cleared"), ph.sem("zero_set")
        ac_ready, t_ready, at_ready = ph.sem("chunk_ready"), ph.sem("transposed_ready"), ph.sem("attention_t_ready")
        u_ready, var_ready, std_ready = ph.sem("unified_ready"), ph.sem("variance_ready"), ph.sem("deviation_ready")
        rms_ready, stats_ready = ph.sem("rms_ready"), ph.sem("stats_ready")
        xg_ready, yg_ready, n_ready = ph.sem("xn_ready"), ph.sem("y_ready"), ph.sem("norm_transposed_ready")
        added, sq_done = ph.sem("attention_added"), ph.sem("squares_summed")
        n_copied, xn_kept, dchain = ph.sem("norm_copied"), ph.sem("xn_kept"), ph.sem("vector_chain")
        block = ph.block()

        @block.sync
        def _(sp):
            sp.dma_start(WU[:, :, :], w_unify.rearrange("(k p) n -> p k n", p=P)).then_inc(w_in, 16)
            sp.dma_start(NW[:, :], norm_w.rearrange("(k p) -> p k", p=P), allow_slow_non_contiguous=True)\
                .then_inc(w_in, 16)
            sp.wait_ge(zero_set, 1)
            rows = DISP.rearrange("(n p r) c -> n p (r c)", p=P, r=4)
            for n in range(rows.shape[0]):
                sp.dma_start(rows[n], ZERO[:, :]).then_inc(cleared, 16)
            sp.wait_ge(cleared, 16 * rows.shape[0])

        def chunks(engine, body):
            with engine.Fori(0, NCH - 1) as n:
                body(n, False)
            body(NCH - 1, True)

        @block.gpsimd
        def _(pool):
            def gather(n):
                for j in range(TC):
                    nc.gpsimd.tensor_copy(
                        AC[:, j, :].rearrange("p (h d) -> p h d", d=D),
                        ATT[:, 1:, :].rearrange("p (h c) x -> p h (c x)", c=NCH)[:, :, bass.ds(n * (TC * D) + j * D, D)])\
                        .then_inc(ac_ready, 1)

            def body(n, last):
                if not last:
                    pool.wait_ge(at_ready, (n + 1) * KC)
                    gather(n + 1)
                pool.wait_ge(xg_ready, n + 1)
                nc.gpsimd.tensor_copy(XN1[:, bass.ds(n * TC, TC), :], XG[:, :, :]).then_inc(xn_kept, 1)

            nc.gpsimd.memset(ZERO[:, :], 0.0).then_inc(zero_set, 1)
            pool.wait_ge(zero_set, 1)
            nc.gpsimd.memset(EPS[:, :], 1e-6).then_inc(zero_set, 1)
            pool.wait_ge(zero_set, 2)
            gather(0)
            pool.wait_ge(ac_ready, TC)
            nc.gpsimd.memset(YT[:, :, 0:1], 0.0).then_inc(zero_set, 1)
            pool.wait_ge(zero_set, 3)
            nc.gpsimd.memset(YT[:, :, T + 1:T + 2], 0.0).then_inc(zero_set, 1)
            pool.wait_ge(zero_set, 4)
            chunks(pool, body)

        @block.tensor
        def _(pe):
            ident = CST[:, IDENT:IDENT + P]

            def unify(n):
                pe.wait_ge(ac_ready, (n + 1) * TC)
                for m in range(KC):
                    for j in range(TC):
                        mm = nc.tensor.transpose(TP[m][:, j * P:(j + 1) * P], AC[:, j, m * P:(m + 1) * P], ident)
                    mm.then_inc(t_ready, 1)
                pe.wait_ge(at_ready, (n + 1) * KC)
                pe.wait_ge(added, n + 1)
                for j in range(TC):
                    for q in range(KC):
                        mm = nc.tensor.matmul(UP[j // 2][:, j % 2 * C:(j % 2 + 1) * C], AT[:, q, j * P:(j + 1) * P],
                                              WU[:, q, :], start=(q == 0), stop=(q == KC - 1))
                mm.then_inc(u_ready, 1)

            def body(n, last):
                if not last:
                    unify(n + 1)
                pe.wait_ge(n_copied, (n + 1) * 2 * KC)
                for g, (src, ready) in enumerate(((XG, xg_ready), (YG, yg_ready))):
                    pe.wait_ge(ready, n + 1)
                    for m in range(KC):
                        for j in range(TC):
                            mm = nc.tensor.transpose(NP[g * KC + m][:, j * P:(j + 1) * P],
                                                     src[:, j, m * P:(m + 1) * P], ident)
                        mm.then_inc(n_ready, 1)

            pe.wait_ge(w_in, 32)
            unify(0)
            chunks(pe, body)

        @block.scalar
        def _(act):
            def copy_attention(n):
                for m in range(KC):
                    act.wait_ge(t_ready, n * KC + m + 1)
                    nc.scalar.copy(AT[:, m, :], TP[m][:, :]).then_inc(at_ready, 1)

            def body(n, last):
                act.wait_ge(var_ready, n + 1)
                nc.scalar.activation(STD[:, :], VAR[:, :], ACT.Sqrt).then_inc(std_ready, 1)
                if not last:
                    act.wait_ge(u_ready, n + 1)
                    copy_attention(n + 1)
                act.wait_ge(xg_ready, n + 1)
                for j in range(TC):
                    nc.scalar.activation(SQ[:, :], XG[:, j, :], ACT.Square, accum_out=MS[:, j:j + 1])\
                        .then_inc(sq_done, 1)
                    act.wait_ge(sq_done, n * TC + j + 1)
                nc.scalar.activation(RMS[:, :], MS[:, :], ACT.Sqrt, bias=EPS[:, :], scale=1.0 / C)\
                    .then_inc(rms_ready, 1)
                for m in range(KC):
                    act.wait_ge(n_ready, n * 2 * KC + m + 1)
                    nc.scalar.copy(XT1[:, m, bass.ds(n * CH, CH)], NP[m][:, :]).then_inc(n_copied, 1)
                for m in range(KC):
                    act.wait_ge(n_ready, n * 2 * KC + KC + m + 1)
                    nc.scalar.activation(YT[:, m, bass.ds(n * CH + 1, CH)], NP[KC + m][:, :], ACT.Copy,
                                         scale=NW[:, m:m + 1]).then_inc(n_copied, 1)

            act.sem_inc(n_copied, 2 * KC)
            act.sem_inc(xn_kept, 1)
            act.wait_ge(w_in, 32)
            act.wait_ge(zero_set, 2)
            copy_attention(0)
            chunks(act, body)

        @block.vector
        def _(dve):
            link = Chain(dve, dchain)
            dve.sem_inc(added, 1)
            with dve.Fori(0, NCH) as n:
                link.start(n * 7)
                dve.wait_ge(u_ready, n + 1)
                for h in range(2):
                    two = X[:, bass.ds(n * TC + 2 * h, 2), :]
                    ins = nc.vector.tensor_tensor(two, UP[h][:, :].rearrange("p (a c) -> p a c", a=2), two, ALU.add)
                link(ins)
                dve.sem_inc(added, 1)
                for j in range(TC):
                    ins = nc.vector.bn_stats(STATS[:, j, :], X[:, bass.ds(n * TC + j, 1), :].rearrange("p a c -> p (a c)"))
                link(ins)
                dve.sem_inc(stats_ready, 1)
                for j in range(TC):
                    ins = nc.vector.bn_aggr(MV[:, j, :], STATS[:, j, :])
                link(ins)
                link(nc.vector.tensor_scalar(VAR[:, :], MV[:, :, 1], LN_EPS, None, ALU.add))
                dve.sem_inc(var_ready, 1)
                dve.wait_ge(std_ready, n + 1)
                link(nc.vector.reciprocal(RSTD[:, :], STD[:, :]))
                dve.wait_ge(n_copied, (n + 1) * 2 * KC)
                dve.wait_ge(xn_kept, n + 1)
                for j in range(TC):
                    ins = nc.vector.tensor_scalar(XG[:, j, :], X[:, bass.ds(n * TC + j, 1), :].rearrange("p a c -> p (a c)"),
                                                  MV[:, j, 0:1], RSTD[:, j:j + 1], ALU.subtract, ALU.mult)
                ins.then_inc(xg_ready, 1)
                dve.wait_ge(rms_ready, n + 1)
                link(nc.vector.reciprocal(RRMS[:, :], RMS[:, :]))
                for j in range(TC):
                    ins = nc.vector.tensor_scalar(YG[:, j, :], XG[:, j, :], RRMS[:, j:j + 1], None, ALU.mult)
                link(ins)
                dve.sem_inc(yg_ready, 1)


def router_phase(nc, rw1, rb1, rw2, rb2, conv_w, conv_b, a, b, CST, XT1, YT, X2T, LG):
    with Phase(nc, "router") as ph:
        W1H, W1L = (ph.sb(f"w1_{part}", [P, KC, HID], F32R) for part in ("high", "low"))
        XH, XL = ([ph.sb(f"xn_{part}{k}", [P, KC, CH], F32R) for k in range(2)] for part in ("high", "low"))
        W2 = ph.sb("w2", [P, MH, E1])
        B1 = ph.sb("b1", [P, MH])
        B2 = ph.sb("b2", [P, E1])
        CW = ph.sb("conv_w", [P, KC, 3])
        CB, AV, BV = (ph.sb(n, [P, KC]) for n in ("conv_b", "a", "b"))
        S = AV
        RH = ph.sb("hidden", [P, 4, CH])
        L4 = RH[:, 3, :]
        W1 = RH[:, :, :].rearrange("p (k a) c -> p k (a c)", k=KC)
        HP = [ph.ps(f"hidden{k}") for k in range(3)]
        LP, SUM_P = ph.ps("logit_parts"), ph.ps("logits")
        w_in, b_in, h_ready, r_done, l4_copied, s_ready, l_copied = (
            ph.sem(n) for n in ("weights_in", "biases_in", "hidden_ready", "relu_done", "logit_parts_copied", "logits_ready", "logits_copied"))
        lp_set, w_split, xh_ready, xl_ready, l_unit = (ph.sem(n) for n in ("logit_parts_cleared", "weights_split",
                                                                          "xn_high_ready", "xn_low_ready",
                                                                          "logit_unit_done"))
        decay_ready, dchain = ph.sem("decay_ready"), ph.sem("vector_chain")
        block = ph.block()

        @block.sync
        def _(sp):
            sp.dma_start(W1, rw1.rearrange("(k p) n -> p k n", p=P)).then_inc(w_in, 16)
            for dst, src in ((CB, conv_b), (AV, a), (BV, b)):
                sp.dma_start(dst[:, :], src.rearrange("(k p) -> p k", p=P), allow_slow_non_contiguous=True)\
                    .then_inc(b_in, 16)
            sp.dma_start(B1[:, :], rb1.rearrange("(m p) -> p m", p=P), allow_slow_non_contiguous=True).then_inc(b_in, 16)
            sp.dma_start(B2[:, :], rb2.rearrange("(o e) -> o e", o=1).to_broadcast([P, E1])).then_inc(b_in, 16)
            sp.dma_start(CW[:, :, :], conv_w.rearrange("(k p) o w -> p k (o w)", p=P)).then_inc(b_in, 16)
            sp.dma_start(W2[:, :, :], rw2.rearrange("(m p) e -> p m e", p=P)).then_inc(b_in, 16)

        @block.gpsimd
        def _(pool):
            with pool.Fori(0, NCH // 2) as i:
                for k in range(2):
                    n = 2 * i + k
                    pool.wait_ge(xh_ready, n + 1)
                    nc.gpsimd.tensor_tensor(XL[k][:, :, :], XT1[:, :, bass.ds(n * CH, CH)],
                                            XH[k][:, :, :].bitcast(F32), ALU.subtract).then_inc(xl_ready, 1)

        @block.tensor
        def _(pe):
            def sum_logits(n):
                pe.wait_ge(l4_copied, n + 1)
                if not isinstance(n, int) or n:
                    pe.wait_ge(l_copied, n)
                for j in range(TC):
                    mm = nc.tensor.matmul(SUM_P[:, j * E1:(j + 1) * E1], L4[:, j * P:(j + 1) * P],
                                          CST[:, SUMCOL:SUMCOL + E1], start=True, stop=True)
                mm.then_inc(s_ready, 1)

            def logits_unit(n, u):
                pe.wait_ge(r_done, n * MH + 4 * u + 4 + 3)
                for g in range(4):
                    mm = nc.tensor.matmul(LP[32 * g:32 * g + E1, :], W2[:, 4 * u + g, :], RH[:, g, :], start=(u == 0),
                                          stop=(u == MH // 4 - 1))
                mm.then_inc(l_unit, 1)

            def body(n, k, first):
                pe.wait_ge(xl_ready, n + 1)
                for m in range(MH):
                    pe.wait_ge(r_done, n * MH + m + 1 + (m < MH % 3))
                    for q in range(KC):
                        mm = products(nc, HP[m % 3][:, :], [w[:, q, m * P:(m + 1) * P] for w in (W1H, W1L)],
                                      [part[k][:, q, :] for part in (XH, XL)], q == 0, q == KC - 1)
                    mm.then_inc(h_ready, 1)
                    if m == 2 and not first:
                        sum_logits(n - 1)
                    if m == 5:
                        logits_unit(n, 0)
                logits_unit(n, 1)

            pe.wait_ge(w_split, 1)
            pe.wait_ge(b_in, 112)
            pe.wait_ge(lp_set, 1)
            body(0, 0, True)
            body(1, 1, False)
            with pe.Fori(0, NCH // 2 - 1) as i:
                for k in range(2):
                    body(2 * i + 2 + k, k, False)
            sum_logits(NCH - 1)

        @block.scalar
        def _(act):
            def high(n, k):
                nc.scalar.copy(XH[k][:, :, :], XT1[:, :, bass.ds(n * CH, CH)]).then_inc(xh_ready, 1)

            def copy_logits(n):
                act.wait_ge(s_ready, n + 1)
                nc.scalar.copy(LG[:, :, bass.ds(n * TC, TC)].rearrange("p e t -> p t e"),
                               SUM_P[:, 0:TC * E1].rearrange("p (t e) -> p t e", e=E1)).then_inc(l_copied, 1)

            def body(n, k, first):
                if not (isinstance(n, int) and n == NCH - 1):
                    high(n + 1, 1 - k)
                for m in range(MH):
                    act.wait_ge(h_ready, n * MH + m + 1)
                    if m % 4 == 0 and not (first and m == 0):
                        act.wait_ge(l_unit, 2 * n + m // 4)
                    nc.scalar.activation(RH[:, m % 4, :], HP[m % 3][:, :], ACT.Relu, bias=B1[:, m:m + 1]).then_inc(r_done, 1)
                    if m == 4 and not first:
                        copy_logits(n - 1)
                act.wait_ge(l_unit, 2 * (n + 1))
                nc.scalar.copy(L4, LP[:, :]).then_inc(l4_copied, 1)

            act.sem_inc(r_done, 3)
            high(0, 0)
            act.wait_ge(b_in, 112)
            nc.scalar.activation(S[:, :], AV[:, :], ACT.Tanh).then_inc(decay_ready, 1)
            act.wait_ge(w_split, 1)
            body(0, 0, True)
            body(1, 1, False)
            with act.Fori(0, NCH // 2 - 2) as i:
                for k in range(2):
                    body(2 * i + 2 + k, k, False)
            for k in range(2):
                body(NCH - 2 + k, k, False)
            copy_logits(NCH - 1)

        @block.vector
        def _(dve):
            link = Chain(dve, dchain)
            nc.vector.memset(LP[:, :], 0.0).then_inc(lp_set, 1)
            dve.wait_ge(w_in, 16)
            split(nc, link, W1, W1H[:, :, :], W1L[:, :, :]).then_inc(w_split, 1)
            dve.wait_ge(b_in, 112)
            dve.wait_ge(decay_ready, 1)
            for k in range(KC):
                x2, y = X2T[:, k, :], YT[:, k, :]
                link(nc.vector.tensor_scalar(x2, y[:, 1:T + 1], BV[:, k:k + 1], None, ALU.mult))
                link(nc.vector.tensor_tensor_scan(x2, S[:, k:k + 1].to_broadcast([P, T]), x2, 0.0, ALU.mult, ALU.add))
                for w in range(3):
                    link(nc.vector.scalar_tensor_tensor(x2, y[:, w:w + T], CW[:, k, w:w + 1], x2, ALU.mult, ALU.add))
                link(nc.vector.scalar_tensor_tensor(x2, XT1[:, k, :], CB[:, k:k + 1], x2, ALU.add, ALU.add))
            dve.wait_ge(l_copied, NCH)
            link(nc.vector.tensor_tensor(LG[:, :, :], LG[:, :, :], B2[:, :].unsqueeze(2).to_broadcast([P, E1, NT]),
                                         ALU.add))


def dispatch_phase(nc, CST, LG, SLOTS, WEIGHTS):
    with Phase(nc, "dispatch") as ph:
        shape = [P, E1, NT]
        FIRST, SECOND, EQ, REST, MASK, RANK = (ph.sb(n, shape) for n in ("first", "second", "eq", "rest", "mask", "rank"))
        BEST1, BEST2, INDEX, POS, BASE, FULL, PROB = (ph.sb(n, [P, NT]) for n in
                                                      ("best1", "best2", "index", "pos", "base", "full", "prob"))
        ranks = Ranks(ph, E1)
        diff_ready, exp_ready, dchain = ph.sem("difference_ready"), ph.sem("exp_ready"), ph.sem("vector_chain")
        block = ph.block()
        iota = CST[:, IOTA:IOTA + E1 * NT].rearrange("p (e t) -> p e t", t=NT)

        @block.scalar
        def _(act):
            act.wait_ge(diff_ready, 1)
            nc.scalar.activation(PROB[:, :], PROB[:, :], ACT.Exp).then_inc(exp_ready, 1)

        @block.tensor
        def _(pe):
            ranks.count(nc, pe, CST, MASK)

        @block.vector
        def _(dve):
            link = Chain(dve, dchain)
            top_two(nc, link, CST, LG, E1, -3.0e38, (FIRST, SECOND, EQ, REST, BEST1, BEST2, INDEX))
            link(nc.vector.tensor_tensor(PROB[:, :], BEST2[:, :], BEST1[:, :], ALU.subtract))
            dve.sem_inc(diff_ready, 1)
            link(nc.vector.tensor_tensor(MASK[:, :, :], FIRST[:, :, :], SECOND[:, :, :], ALU.add))
            dve.sem_inc(ranks.mask_ready, 1)
            ranks.finish(nc, dve, link, CST, RANK)
            dve.wait_ge(exp_ready, 1)
            link(nc.vector.tensor_scalar(WEIGHTS[:, 0, :], PROB[:, :], 1.0, None, ALU.add))
            link(nc.vector.reciprocal(WEIGHTS[:, 0, :], WEIGHTS[:, 0, :]))
            link(nc.vector.tensor_tensor(WEIGHTS[:, 1, :], PROB[:, :], WEIGHTS[:, 0, :], ALU.mult))
            for k, hot in enumerate((FIRST, SECOND)):
                for dst, what in ((POS, RANK[:, :, :]), (BASE, iota)):
                    link(nc.vector.tensor_tensor(EQ[:, :, :], hot[:, :, :], what, ALU.mult))
                    link(nc.vector.tensor_reduce(dst[:, :], EQ[:, :, :].rearrange("p e t -> p t e"), AX.X, ALU.add))
                link(nc.vector.tensor_scalar(BASE[:, :], BASE[:, :], float(CAP), None, ALU.mult))
                link(nc.vector.tensor_scalar(FULL[:, :], POS[:, :], CAP - 0.5, float(1 << 20), ALU.is_ge, ALU.mult))
                link(nc.vector.tensor_tensor(INDEX[:, :], BASE[:, :], POS[:, :], ALU.add))
                link(nc.vector.tensor_tensor(INDEX[:, :], INDEX[:, :], FULL[:, :], ALU.add))
                link(nc.vector.tensor_copy(SLOTS[:, k, :], INDEX[:, :]))
                link(nc.vector.tensor_scalar(INDEX[:, :], POS[:, :], CAP - 1.0, None, ALU.min))
                link(nc.vector.tensor_tensor(INDEX[:, :], INDEX[:, :], BASE[:, :], ALU.add))
                link(nc.vector.tensor_copy(SLOTS[:, 2 + k, :], INDEX[:, :]))
                link(nc.vector.tensor_scalar(FULL[:, :], POS[:, :], CAP - 0.5, None, ALU.is_lt))
                link(nc.vector.tensor_tensor(WEIGHTS[:, k, :], WEIGHTS[:, k, :], FULL[:, :], ALU.mult))


def mlp_phase(nc, mlp_norm_w, w_gate, b_gate, w_up, b_up, w_down, b_down, CST, X2T, X, XN1, SLOTS, DISP):
    with Phase(nc, "mlp") as ph:
        WH, WL, DH, DL = (ph.sb(n, s, F32R) for n, s in (("w_in_high", [P, 2 * KC, HID]), ("w_in_low", [P, 2 * KC, HID]),
                                                         ("w_down_high", [P, MH, C]), ("w_down_low", [P, MH, C])))
        BG, BU = ph.sb("b_gate", [P, MH]), ph.sb("b_up", [P, MH])
        BD = ph.sb("b_down", [P, C])
        NW = ph.sb("norm_w", [P, KC])
        EPS = ph.sb("eps", [P, 1])
        XC = ph.sb("x2_chunk", [P, KC, CH])
        RMS = ph.sb("rms", [P, CH])
        ZF = ph.sb("z", [P, KC, CH])
        SQ = ZF
        ZH, ZL = (ph.sb(f"z_{part}", [P, KC, CH], F32R) for part in ("high", "low"))
        GG = ph.sb("silu", [P, 2, CH])
        G = [GG[:, k, :] for k in range(2)]
        HH, HL = ph.sb("hidden_high", [P, MH, CH], F32R), ph.sb("hidden_low", [P, MH, CH], F32R)
        WF = [XC[:, :, :].rearrange("p k n -> p (k n)"), GG[:, :, :].rearrange("p k n -> p (k n)")]
        gate, up = (w.rearrange("(k p) n -> k p n", p=P) for w in (w_gate, w_up))
        down = w_down.rearrange("(m p) n -> p m n", p=P)
        PIECES = [(w[q].unsqueeze(1), WH[:, g * KC + q:g * KC + q + 1, :], WL[:, g * KC + q:g * KC + q + 1, :])
                  for g, w in enumerate((gate, up)) for q in range(KC)]
        PIECES += [(down[:, m:m + MH // 2, :], DH[:, m:m + MH // 2, :], DL[:, m:m + MH // 2, :]) for m in (0, MH // 2)]
        GP = [ph.ps(f"gate{k}") for k in range(2)]
        UP = [ph.ps(f"up{k}") for k in range(2)]
        OP = [ph.ps(f"out{k}") for k in range(2)]
        QP = ph.ps("squares")
        w_in = [ph.sem(f"weights_in{k}") for k in range(2)]
        xc_in = ph.sem("x2_in")
        b_in = ph.sem("biases_in")
        w_split = ph.sem("weights_split")
        eps_set, sq_ready, sum_ready, rms_ready, z_ready = (ph.sem(n) for n in
                                                            ("eps_set", "squares_ready", "sums_ready", "rms_ready",
                                                             "z_ready"))
        g_ready, u_ready, s_done, h_done, h_split, o_ready, o_used = (ph.sem(n) for n in
                                                                      ("gate_ready", "up_ready", "silu_done",
                                                                       "hidden_done", "hidden_split", "out_ready",
                                                                       "out_used"))
        scattered, dchain = ph.sem("rows_written"), ph.sem("vector_chain")
        block = ph.block()

        def chunks(engine, body):
            with engine.Fori(0, NCH - 1) as n:
                body(n, False)
            body(NCH - 1, True)

        @block.sync
        def _(sp):
            for dst, src in ((BG, b_gate), (BU, b_up)):
                sp.dma_start(dst[:, :], src.rearrange("(m p) -> p m", p=P), allow_slow_non_contiguous=True)\
                    .then_inc(b_in, 16)
            sp.dma_start(NW[:, :], mlp_norm_w.rearrange("(k p) -> p k", p=P), allow_slow_non_contiguous=True)\
                .then_inc(b_in, 16)
            sp.dma_start(BD[:, :], b_down.rearrange("(a n) -> a n", a=1).to_broadcast([P, C])).then_inc(b_in, 16)
            for n, (source, high, _) in enumerate(PIECES):
                if n >= 2:
                    sp.wait_ge(w_split, n - 1)
                sp.dma_start(WF[n % 2].rearrange("p (a n) -> p a n", a=high.shape[1]), source).then_inc(w_in[n % 2], 16)
            sp.wait_ge(w_split, len(PIECES) - 1)
            with sp.Fori(0, NCH) as n:
                sp.wait_ge(o_used, n + 1)
                sp.dma_start(XC[:, :, :], X2T[:, :, bass.ds(n * CH, CH)]).then_inc(xc_in, 16)

        @block.gpsimd
        def _(pool):
            nc.gpsimd.memset(EPS[:, :], 1e-6).then_inc(eps_set, 1)
            for t in range(NT):
                for k in range(2):
                    pool.indirect_dma_start(DISP, bass.IndirectOffsetOnAxis(ap=SLOTS[:, k, t:t + 1], axis=0),
                                            XN1[:, t, :], None, bounds_check=E1 * CAP - 1, oob_is_err=False)\
                        .then_inc(scattered, 16)
            pool.wait_ge(scattered, 2 * NT * 16)

        @block.tensor
        def _(pe):
            def sum_squares(n):
                pe.wait_ge(sq_ready, n + 1)
                for q in range(KC):
                    mm = nc.tensor.matmul(QP[:, :], CST[:, ONES:ONES + P], SQ[:, q, :], start=(q == 0),
                                          stop=(q == KC - 1))
                mm.then_inc(sum_ready, 1)

            def body(n, last):
                pe.wait_ge(z_ready, n + 1)
                for m in range(MH):
                    pe.wait_ge(h_done, n * MH + m + 1)
                    for g, (bank, ready) in enumerate(((GP, g_ready), (UP, u_ready))):
                        for q in range(KC):
                            w = [part[:, g * KC + q, m * P:(m + 1) * P] for part in (WH, WL)]
                            mm = products(nc, bank[m % 2][:, :], w, [part[:, q, :] for part in (ZH, ZL)],
                                          q == 0, q == KC - 1)
                        mm.then_inc(ready, 1)
                if not last:
                    sum_squares(n + 1)
                pe.wait_ge(h_split, (n + 1) * MH + 2)
                pe.wait_ge(o_used, n + 1)
                pe.wait_ge(xc_in, (n + 1) * 16)
                for j in range(TC):
                    o = OP[j // 2][:, j % 2 * C:(j % 2 + 1) * C]
                    for m in range(MH):
                        products(nc, o, [part[:, m, j * P:(j + 1) * P] for part in (HH, HL)],
                                 [part[:, m, :] for part in (DH, DL)], m == 0, m == MH - 1)
                    for q in range(KC):
                        mm = nc.tensor.matmul(o[:, q * P:(q + 1) * P], XC[:, q, j * P:(j + 1) * P],
                                              CST[:, IDENT:IDENT + P], start=False, stop=True, skip_group_check=True)
                    mm.then_inc(o_ready, 1)

            sum_squares(0)
            pe.wait_ge(w_split, len(PIECES))
            chunks(pe, body)

        @block.scalar
        def _(act):
            def squares(n):
                if not isinstance(n, int) or n:
                    act.wait_ge(z_ready, n)
                nc.scalar.activation(SQ[:, :, :], X2T[:, :, bass.ds(n * CH, CH)], ACT.Square).then_inc(sq_ready, 1)

            def roots(n):
                act.wait_ge(sum_ready, n + 1)
                nc.scalar.activation(RMS[:, :], QP[:, :], ACT.Sqrt, bias=EPS[:, :], scale=1.0 / C).then_inc(rms_ready, 1)

            def body(n, last):
                for m in range(MH):
                    act.wait_ge(g_ready, n * MH + m + 1)
                    act.wait_ge(h_split, n * MH + m + 1)
                    nc.scalar.activation(G[m % 2], GP[m % 2][:, :], ACT.Silu, bias=BG[:, m:m + 1])\
                        .then_inc(s_done, 1)
                    if m == 0 and not last:
                        squares(n + 1)
                if not last:
                    roots(n + 1)

            act.sem_inc(h_done, 2)
            act.sem_inc(h_split, 2)
            squares(0)
            act.wait_ge(eps_set, 1)
            roots(0)
            act.wait_ge(b_in, 64)
            chunks(act, body)

        @block.vector
        def _(dve):
            link = Chain(dve, dchain)

            def split_z(n):
                dve.wait_ge(rms_ready, n + 1)
                link(nc.vector.reciprocal(RMS[:, :], RMS[:, :]))
                for q in range(KC):
                    ins = nc.vector.scalar_tensor_tensor(ZF[:, q, :], X2T[:, q, bass.ds(n * CH, CH)], NW[:, q:q + 1],
                                                         RMS[:, :], ALU.mult, ALU.mult)
                link(ins)
                split(nc, link, ZF[:, :, :], ZH[:, :, :], ZL[:, :, :]).then_inc(z_ready, 1)

            def body(n, last):
                for m in range(MH):
                    dve.wait_ge(s_done, n * MH + m + 1)
                    dve.wait_ge(u_ready, n * MH + m + 1)
                    whole = G[m % 2]
                    nc.vector.scalar_tensor_tensor(whole, UP[m % 2][:, :], BU[:, m:m + 1], G[m % 2],
                                                   ALU.add, ALU.mult).then_inc(h_done, 1)
                    dve.wait_ge(h_done, n * MH + m + 3)
                    split(nc, link, whole, HH[:, m, :], HL[:, m, :]).then_inc(h_split, 1)
                if not last:
                    split_z(n + 1)
                for h in range(2):
                    dve.wait_ge(o_ready, n * TC + 2 * h + 2)
                    two = X[:, bass.ds(n * TC + 2 * h, 2), :]
                    ins = nc.vector.tensor_tensor(two, OP[h][:, :].rearrange("p (a c) -> p a c", a=2), two, ALU.add)
                link(ins)
                dve.sem_inc(o_used, 1)
                xs = X[:, bass.ds(n * TC, TC), :]
                link(nc.vector.tensor_tensor(xs, xs, BD[:, :].unsqueeze(1).to_broadcast([P, TC, C]), ALU.add))

            dve.sem_inc(o_used, 1)
            for n, (_, high, low) in enumerate(PIECES):
                dve.wait_ge(w_in[n % 2], 16 * (n // 2 + 1))
                whole = WF[n % 2].rearrange("p (a n) -> p a n", a=high.shape[1])
                split(nc, link, whole, high, low).then_inc(w_split, 1)
                if n == 1:
                    dve.wait_ge(b_in, 64)
                    split_z(0)
            first, per_chunk = link.n, MH + 3 + 2
            with dve.Fori(0, NCH - 1) as n:
                link.start(first + n * per_chunk)
                body(n, False)
            link.start(first + (NCH - 1) * per_chunk)
            body(NCH - 1, True)


def expert_phase(nc, ew1, eb1, ew2, eb2, CST, V, DISP, EOUT):
    NS = CAP // P
    with Phase(nc, "experts") as ph:
        S1, S2 = ph.sb("w1_whole", [P, KC, HID]), ph.sb("w2_whole", [P, MH, C])
        W1 = [[ph.sb(f"w1_{part}{k}", [P, KC, HID], F32R) for part in ("high", "low")] for k in range(2)]
        W2 = [[ph.sb(f"w2_{part}{k}", [P, MH, C], F32R) for part in ("high", "low")] for k in range(2)]
        B1 = [ph.sb(f"b1_{k}", [P, MH]) for k in range(2)]
        B2 = [ph.sb(f"b2_{k}", [P, C]) for k in range(2)]
        R = [V[:, k * NS:(k + 1) * NS, :] for k in range(2)]
        O = [V[:, 2 * NS + k * TC:2 * NS + (k + 1) * TC, :] for k in range(2)]
        HF = [V[:, 3 * NS + 2 * k:3 * NS + 2 * k + 2, :].rearrange("p a c -> p (a c)") for k in range(2)]
        RT = [ph.sb(f"rows_t_{part}", [P, KC, CH], F32R) for part in ("high", "low")]
        HH, HL = (ph.sb(f"hidden_{part}", [P, MH, CH], F32R) for part in ("high", "low"))
        TP = [ph.ps(f"transposed{k}") for k in range(KC)]
        HP = [ph.ps(f"hidden{k}") for k in range(2)]
        OP = [ph.ps(f"out{k}") for k in range(2)]
        s1_in, s2_in, w1_split, w2_split = (ph.sem(n) for n in ("w1_in", "w2_in", "w1_split", "w2_split"))
        loaded = [ph.sem(f"expert_in{k}") for k in range(2)]
        stored = [ph.sem(f"out_stored{k}") for k in range(2)]
        t_ready, rth_ready, rt_ready, h_ready, r_done, h_split, o_ready, o_copied, dchain = (
            ph.sem(n) for n in ("transposed_ready", "rows_high_ready", "rows_low_ready", "hidden_ready", "relu_done",
                                "hidden_split", "out_ready", "out_copied", "vector_chain"))
        block = ph.block()
        LOAD = 3 * 16

        def experts(engine, body):
            with engine.Fori(0, E1 // 2 - 1) as i:
                for k in range(2):
                    body(2 * i + k, i, k, False)
            for k in range(2):
                body(E1 - 2 + k, E1 // 2 - 1, k, k == 1)

        @block.sync
        def _(sp):
            rows = EOUT.rearrange("(n p) c -> p n c", p=P)

            def load_w1(e):
                sp.dma_start(S1[:, :, :], ew1.rearrange("e (k p) n -> p e k n", p=P)[:, bass.ds(e, 1)]
                             .rearrange("p e k n -> p (e k) n")).then_inc(s1_in, 16)

            def load_w2(e):
                sp.dma_start(S2[:, :, :], ew2.rearrange("e (m p) n -> p e m n", p=P)[:, bass.ds(e, 1)]
                             .rearrange("p e m n -> p (e m) n")).then_inc(s2_in, 16)

            def load_rows(e, k):
                sp.dma_start(R[k][:, :, :], DISP.rearrange("(n p) c -> p n c", p=P)[:, bass.ds(e * NS, NS), :])\
                    .then_inc(loaded[k], 16)
                sp.dma_start(B1[k][:, :], eb1.rearrange("e (m p) -> p e m", p=P)[:, bass.ds(e, 1)]
                             .rearrange("p e m -> p (e m)"), allow_slow_non_contiguous=True).then_inc(loaded[k], 16)
                sp.dma_start(B2[k][:, :], eb2[bass.ds(e, 1), :].to_broadcast([P, C])).then_inc(loaded[k], 16)

            def store(e, h):
                sp.wait_ge(o_copied, e * 4 + 2 * h + 4)
                sp.dma_start(rows[:, bass.ds(e * NS + h * TC, TC), :], O[h][:, :, :]).then_inc(stored[h], 16)

            load_w1(0)
            load_rows(0, 0)
            load_w2(0)
            load_rows(1, 1)
            sp.wait_ge(w1_split, 1)
            load_w1(1)
            sp.wait_ge(w2_split, 1)
            load_w2(1)
            with sp.Fori(0, E1 // 2 - 1) as i:
                for k in range(2):
                    e = 2 * i + k
                    sp.wait_ge(w1_split, e + 2)
                    load_w1(e + 2)
                    store(e, 0)
                    sp.wait_ge(w2_split, e + 2)
                    load_w2(e + 2)
                    store(e, 1)
                    load_rows(e + 2, k)
            for e in (E1 - 2, E1 - 1):
                for h in range(2):
                    store(e, h)
            for h in range(2):
                sp.wait_ge(stored[h], (E1 + 1) * 16)

        @block.tensor
        def _(pe):
            def turn(k, h):
                for m in range(KC):
                    for j in range(TC):
                        mm = nc.tensor.transpose(TP[m][:, j * P:(j + 1) * P], R[k][:, h * TC + j, m * P:(m + 1) * P],
                                                 CST[:, IDENT:IDENT + P])
                    mm.then_inc(t_ready, 1)

            def body(e, i, k, last):
                for h in range(2):
                    g = 2 * e + h
                    if h == 0:
                        pe.wait_ge(w1_split, e + 1)
                    pe.wait_ge(rt_ready, (g + 1) * KC)
                    for m in range(MH):
                        pe.wait_ge(r_done, g * MH + m + 1)
                        for q in range(KC):
                            mm = products(nc, HP[m % 2][:, :], [w[:, q, m * P:(m + 1) * P] for w in W1[k]],
                                          [r[:, q, :] for r in RT], q == 0, q == KC - 1)
                        mm.then_inc(h_ready, 1)
                    if h == 0:
                        turn(k, 1)
                        pe.wait_ge(w2_split, e + 1)
                    elif not last:
                        pe.wait_ge(loaded[1 - k], (i + k + 1) * LOAD)
                        turn(1 - k, 0)
                    pe.wait_ge(h_split, (g + 1) * MH + 2)
                    for j in range(TC):
                        if j % 2 == 0:
                            pe.wait_ge(o_copied, g * 2 + j // 2 + 1)
                        for m in range(MH):
                            mm = products(nc, OP[j // 2][:, j % 2 * C:(j % 2 + 1) * C],
                                          [part[:, m, j * P:(j + 1) * P] for part in (HH, HL)],
                                          [w[:, m, :] for w in W2[k]], m == 0, m == MH - 1)
                        if j % 2:
                            mm.then_inc(o_ready, 1)

            pe.wait_ge(loaded[0], LOAD)
            turn(0, 0)
            experts(pe, body)

        @block.scalar
        def _(act):
            def high_rows(g):
                for m in range(KC):
                    act.wait_ge(t_ready, g * KC + m + 1)
                    nc.scalar.copy(RT[0][:, m, :], TP[m][:, :]).then_inc(rth_ready, 1)

            def body(e, i, k, last):
                for h in range(2):
                    g = 2 * e + h
                    for m in range(MH):
                        act.wait_ge(h_ready, g * MH + m + 1)
                        act.wait_ge(h_split, g * MH + m + 1)
                        nc.scalar.activation(HF[m % 2], HP[m % 2][:, :], ACT.Relu, bias=B1[k][:, m:m + 1])\
                            .then_inc(r_done, 1)
                    if not (last and h):
                        high_rows(g + 1)
                        if h:
                            act.wait_ge(loaded[1 - k], (i + k + 1) * LOAD)

            act.sem_inc(r_done, 2)
            act.sem_inc(h_split, 2)
            for h in range(2):
                act.sem_inc(stored[h], 16)
            high_rows(0)
            act.wait_ge(loaded[0], LOAD)
            experts(act, body)

        @block.vector
        def _(dve):
            link = Chain(dve, dchain)

            def low_rows(g):
                for m in range(KC):
                    dve.wait_ge(rth_ready, g * KC + m + 1)
                    nc.vector.tensor_tensor(RT[1][:, m, :], TP[m][:, :], RT[0][:, m, :].bitcast(F32), ALU.subtract)\
                        .then_inc(rt_ready, 1)

            def split_weights(e, k, h):
                arrived, whole, parts, ready = ((s1_in, S1, W1, w1_split), (s2_in, S2, W2, w2_split))[h]
                dve.wait_ge(arrived, (e + 1) * 16)
                split(nc, link, whole[:, :, :], parts[k][0][:, :, :], parts[k][1][:, :, :]).then_inc(ready, 1)

            def body(e, i, k, last):
                for h in range(2):
                    g = 2 * e + h
                    for m in range(MH):
                        dve.wait_ge(r_done, g * MH + m + 3)
                        split(nc, link, HF[m % 2], HH[:, m, :], HL[:, m, :]).then_inc(h_split, 1)
                    if not (last and h):
                        low_rows(g + 1)
                    if not last:
                        split_weights(e + 1, 1 - k, h)
                    for a in range(2):
                        dve.wait_ge(stored[h], (e + 1) * 16)
                        dve.wait_ge(o_ready, g * 2 + a + 1)
                        nc.vector.tensor_tensor(O[h][:, 2 * a:2 * a + 2, :],
                                                OP[a][:, :].rearrange("p (a c) -> p a c", a=2),
                                                B2[k][:, :].unsqueeze(1).to_broadcast([P, 2, C]), ALU.add)\
                            .then_inc(o_copied, 1)
                if not last:
                    dve.wait_ge(loaded[1 - k], (i + k + 1) * LOAD)

            dve.sem_inc(o_copied, 2)
            split_weights(0, 0, 0)
            low_rows(0)
            split_weights(0, 0, 1)
            dve.wait_ge(loaded[0], LOAD)
            first, per_expert = link.n, 2 * MH + 2
            with dve.Fori(0, E1 // 2 - 1) as i:
                link.start(first + i * (2 * per_expert))
                for k in range(2):
                    body(2 * i + k, i, k, False)
            link.start(first + (E1 - 2) * per_expert)
            for k in range(2):
                body(E1 - 2 + k, E1 // 2 - 1, k, k == 1)


def combine_phase(nc, SLOTS, WEIGHTS, EOUT, X, out):
    NR = 4
    with Phase(nc, "combine") as ph:
        G = [ph.sb(f"rows{k}", [P, 2, C]) for k in range(NR)]
        gathered = [ph.sem(f"rows_in{k}") for k in range(NR)]
        added, first, stored = ph.sem("rows_added"), ph.sem("first_added"), ph.sem("out_stored")
        block = ph.block()

        @block.gpsimd
        def _(pool):
            for t in range(NT):
                if t >= NR:
                    pool.wait_ge(added, t - NR + 1)
                for k in range(2):
                    pool.indirect_dma_start(G[t % NR][:, k, :], None, EOUT,
                                            bass.IndirectOffsetOnAxis(ap=SLOTS[:, 2 + k, t:t + 1], axis=0),
                                            bounds_check=E1 * CAP - 1, oob_is_err=False).then_inc(gathered[t % NR], 16)

        @block.vector
        def _(dve):
            for t in range(NT):
                dve.wait_ge(gathered[t % NR], 32 * (t // NR + 1))
                for k in range(2):
                    ins = nc.vector.scalar_tensor_tensor(X[:, t, :], G[t % NR][:, k, :], WEIGHTS[:, k, t:t + 1],
                                                         X[:, t, :], ALU.mult, ALU.add)
                    if k == 0:
                        ins.then_inc(first, 1)
                        dve.wait_ge(first, t + 1)
                ins.then_inc(added, 1)

        @block.sync
        def _(sp):
            rows = out.rearrange("a (n p) c -> p (a n) c", p=P)
            for n in range(NCH):
                sp.wait_ge(added, (n + 1) * TC)
                sp.dma_start(rows[:, n * TC:(n + 1) * TC, :], X[:, n * TC:(n + 1) * TC, :]).then_inc(stored, 16)
            sp.wait_ge(stored, NCH * 16)


def build(nc, ins, out):
    with ExitStack() as whole:
        def sb(name, shape, dt=F32, stack=whole, side="left"):
            return stack.enter_context(nc.sbuf_tensor(name, shape, dt, side=side))

        q_scratch = nc.dram_tensor("q_scratch", (2, C, T), F32).ap()
        k_scratch = nc.dram_tensor("k_scratch", (2, C, T), F32).ap()
        DISP = nc.dram_tensor("expert_rows", (E1 * CAP, C), F32).ap()
        EOUT = nc.dram_tensor("expert_out", (E1 * CAP, C), F32).ap()
        L0, L1 = (lambda name: ins["L0_" + name]), (lambda name: ins["L1_" + name])

        CST = sb("constants", [P, EXPAND])
        X = sb("residual", [P, NT, C])
        V = sb("values", [P, NT, C])
        with ExitStack() as stack:
            XN = sb("xn", [P, NT, C], stack=stack)
            XNT = sb("xn_t", [P, KC, T], stack=stack)
            SC = sb("gate_scores", [P, E0, NT], stack=stack)
            front_phase(nc, L0("attn_x")[0], L0("attn_W_down"),
                        (L0("attn_toqueries"), L0("attn_tokeys"), L0("attn_tovalues")), L0("ffn_wg"), L0("ffn_bg"),
                        ins["constants"], CST, X, XN, XNT, V, SC, q_scratch, k_scratch)
            MASKT = sb("expert_mask_t", [E0, T], BF16, stack=stack)
            select_phase(nc, CST, SC, MASKT)
            ffn0_phase(nc, L0("ffn_w1"), L0("ffn_b1"), L0("ffn_w2"), L0("ffn_b2"), L0("ffn_gamma"), L0("ffn_beta"),
                       L0("attn_b_unify"), ins["constants"], MASKT, X, XN, XNT)
        LG = sb("router_logits", [P, E1, NT])
        SLOTS = sb("slots", [P, 4, NT], I32)
        WEIGHTS = sb("expert_weights", [P, 2, NT])
        XN1 = V
        with ExitStack() as left:
            with ExitStack() as right, ExitStack() as top:
                with ExitStack() as attention:
                    ATT = sb("attention", [P, 1 + HEADS * NCH, TC * D], stack=attention, side="right")
                    attention_phase(nc, q_scratch, k_scratch, V, ATT, CST)
                    XT1 = sb("xn1_t", [P, KC, T], stack=left)
                    YT = sb("y_t", [P, KC, T + 2], stack=top)
                    unify_phase(nc, L0("attn_W_unify"), L1("attn_norm_w"), CST, ATT, X, XN1, XT1, YT, DISP)
                X2T = sb("x2_t", [P, KC, T], stack=right, side="right")
                router_phase(nc, L1("ffn_rw1"), L1("ffn_rb1"), L1("ffn_rw2"), L1("ffn_rb2"), L1("attn_conv_w"),
                             L1("attn_conv_b"), L1("attn_a"), L1("attn_b"), CST, XT1, YT, X2T, LG)
                top.close()
                dispatch_phase(nc, CST, LG, SLOTS, WEIGHTS)
                left.close()
                mlp_phase(nc, L1("attn_mlp_norm_w"), L1("attn_w_gate"), L1("attn_b_gate"), L1("attn_w_up"),
                          L1("attn_b_up"), L1("attn_w_down"), L1("attn_b_down"), CST, X2T, X, XN1, SLOTS, DISP)
        expert_phase(nc, L1("ffn_ew1"), L1("ffn_eb1"), L1("ffn_ew2"), L1("ffn_eb2"), CST, V, DISP, EOUT)
        combine_phase(nc, SLOTS, WEIGHTS, EOUT, X, out)


def constants():
    import numpy as np

    p = np.arange(P)[:, None]
    c = np.zeros((P, CONSTS), np.float32)
    c[:, IDENT:IDENT + P] = p == np.arange(P)
    c[:, SUMCOL:SUMCOL + D + 1] = p % 32 == np.arange(D + 1)
    c[:, DIAG8:DIAG8 + 8] = p // D == np.arange(8)
    c[:, BEFORE:BEFORE + P] = p < np.arange(P)
    c[:, ONES:ONES + P] = 1
    c[:, RESET:RESET + E0 * NT] = np.arange(E0 * NT) % NT != 0
    c[:, IOTA:IOTA + E0 * NT] = np.arange(E0 * NT) // NT
    m, q = np.arange(F0) // P, np.arange(F0) % P
    c[:, EXPAND:EXPAND + F0] = p == 2 * m + q // (F0 // E0)
    return c


def kernel(**inputs):
    import numpy as np
    import concourse.bacc as bacc
    from concourse.bass_utils import run_bass_kernel_spmd

    nc = bacc.Bacc("TRN2", target_bir_lowering=False, num_devices=1)
    arrays = {name: np.ascontiguousarray(a) for name, a in inputs.items()}
    arrays["constants"] = constants()
    arrays = {f"in_{name}": a for name, a in arrays.items()}
    ins = {name[3:]: nc.dram_tensor(name, a.shape, mybir.dt.from_np(a.dtype), kind="ExternalInput").ap()
           for name, a in arrays.items()}
    out = nc.dram_tensor("out_0", (1, T, C), F32, kind="ExternalOutput").ap()
    build(nc, ins, out)
    result = run_bass_kernel_spmd(nc, [arrays], core_ids=[0])
    return result.results[0]["out_0"]
```
